# Optimizing a Trainium2 kernel written in Bass

```python
import numpy as np
import jax
import jax.numpy as jnp

def _softmax(x, axis=-1):
    return jax.nn.softmax(x, axis=axis)

def _gelu(x):
    return jax.nn.gelu(x, approximate=True)

def _silu(x):
    return jax.nn.silu(x)

def _sigmoid(x):
    return jax.nn.sigmoid(x)

def _layernorm(x, axis=-1, eps=1e-05):
    m = jnp.mean(x, axis=axis, keepdims=True)
    v = jnp.var(x, axis=axis, keepdims=True)
    return (x - m) / jnp.sqrt(v + eps)

def _scatter_add(tgt, idx, src, axis=0):
    return tgt.at[idx].add(src)

def _segment_sum(src, seg, n):
    return jax.ops.segment_sum(src, seg, n)
kernel_name = 'mk_xattn_seq_d1_seqx_r8_e6c2ed'

def setup_inputs(seed: int=0):
    np.random.seed(seed)
    _w = jnp.asarray

    def _rec_inputs():
        import jax
        import jax.numpy as jnp
        _rk = jax.random.key(seed)
        x = -0.0002928 + 1 * jax.random.normal(jax.random.fold_in(_rk, 1), (16, 100, 128), jnp.float32)
        _lenS = 100 - jax.random.randint(jax.random.fold_in(_rk, 7), (16,), 0, max(1, 100 // 4) + 1, jnp.int32)
        _lenS2 = 1444 - jax.random.randint(jax.random.fold_in(_rk, 8), (16,), 0, max(1, 1444 // 4) + 1, jnp.int32)
        _ctx_1024P = jax.random.normal(jax.random.fold_in(_rk, 11), (16, 16, 128), jnp.float32)
        _ctx_1024c = jax.random.dirichlet(jax.random.fold_in(_rk, 511), 0.3 * jnp.ones((16,), jnp.float32), (16, 1444))
        _ctx_1024t = jnp.einsum('bsk,bkd->bsd', _ctx_1024c, _ctx_1024P)
        _ctx_1024t = _ctx_1024t * jax.lax.rsqrt(jnp.mean(jnp.square(_ctx_1024t)) + 1e-12) * 0.953939
        ctx_1024 = -1.39393e-06 + 0.999914 * (_ctx_1024t + 0.3 * jax.random.normal(jax.random.fold_in(_rk, 611), (16, 1444, 128), jnp.float32))
        return (x, ctx_1024)
    x, ctx_1024 = _rec_inputs()

    def _L0_xattn_setup():
        import jax, jax.numpy as jnp
        import numpy as np
        B, L, D_E = (2, 256, 128)
        H, D_Q = (16, 64)
        EPS = 1e-05
        key = jax.random.key(seed)
        ks = jax.random.split(key, 12)
        s_in = 1.0 / np.sqrt(D_E)
        s_mid = 1.0 / np.sqrt(H * D_Q)
        return {'pre_q': jax.random.normal(ks[0], (B, L, D_E), jnp.float32), 'pre_k': jax.random.normal(ks[1], (B, L, D_E), jnp.float32), 'Wq': jax.random.normal(ks[2], (D_E, H * D_Q), jnp.float32) * s_in, 'bq': jnp.zeros((H * D_Q,), jnp.float32), 'Wk': jax.random.normal(ks[3], (D_E, H * D_Q), jnp.float32) * s_in, 'bk': jnp.zeros((H * D_Q,), jnp.float32), 'Wv': jax.random.normal(ks[4], (D_E, H * D_Q), jnp.float32) * s_in, 'bv': jnp.zeros((H * D_Q,), jnp.float32), 'Wo': jax.random.normal(ks[5], (H * D_Q, D_E), jnp.float32) * s_mid, 'bo': jnp.zeros((D_E,), jnp.float32), 'gamma': jnp.ones((D_E,), jnp.float32), 'beta': jnp.zeros((D_E,), jnp.float32)}
    _L0_xattn_all = _L0_xattn_setup()
    _L0_xattn_in = {k: v for k, v in _L0_xattn_all.items() if k in ('Wq', 'bq', 'Wk', 'bk', 'Wv', 'bv', 'Wo', 'bo', 'gamma', 'beta')}
    del _L0_xattn_all
    return {'x': x, 'ctx_1024': ctx_1024, 'L0_xattn_Wq': _L0_xattn_in['Wq'], 'L0_xattn_bq': _L0_xattn_in['bq'], 'L0_xattn_Wk': _L0_xattn_in['Wk'], 'L0_xattn_bk': _L0_xattn_in['bk'], 'L0_xattn_Wv': _L0_xattn_in['Wv'], 'L0_xattn_bv': _L0_xattn_in['bv'], 'L0_xattn_Wo': _L0_xattn_in['Wo'], 'L0_xattn_bo': _L0_xattn_in['bo'], 'L0_xattn_gamma': _L0_xattn_in['gamma'], 'L0_xattn_beta': _L0_xattn_in['beta']}

def reference(x, ctx_1024, L0_xattn_Wq, L0_xattn_bq, L0_xattn_Wk, L0_xattn_bk, L0_xattn_Wv, L0_xattn_bv, L0_xattn_Wo, L0_xattn_bo, L0_xattn_gamma, L0_xattn_beta):
    import jax
    import jax.numpy as jnp

    def _L0_xattn_ref(pre_q, pre_k, Wq, bq, Wk, bk, Wv, bv, Wo, bo, gamma, beta):
        import jax, jax.numpy as jnp
        import numpy as np
        B, L, D_E = (2, 256, 128)
        H, D_Q = (16, 64)
        EPS = 1e-05
        b, ql, _ = pre_q.shape
        kl = pre_k.shape[1]
        q = (pre_q @ Wq + bq).reshape(b, ql, H, D_Q)
        k = (pre_k @ Wk + bk).reshape(b, kl, H, D_Q)
        v = (pre_k @ Wv + bv).reshape(b, kl, H, D_Q)
        scores = jnp.einsum('bqhd,bkhd->bhqk', q, k) / jnp.sqrt(jnp.float32(D_Q))
        attn = jax.nn.softmax(scores, axis=-1)
        ctx = jnp.einsum('bhqk,bkhd->bqhd', attn, v).reshape(b, ql, H * D_Q)
        out = ctx @ Wo + bo
        x = pre_q + out
        mu = jnp.mean(x, axis=-1, keepdims=True)
        var = jnp.mean(jnp.square(x - mu), axis=-1, keepdims=True)
        return (x - mu) * jax.lax.rsqrt(var + EPS) * gamma + beta
    x = _L0_xattn_ref(x, ctx_1024, L0_xattn_Wq, L0_xattn_bq, L0_xattn_Wk, L0_xattn_bk, L0_xattn_Wv, L0_xattn_bv, L0_xattn_Wo, L0_xattn_bo, L0_xattn_gamma, L0_xattn_beta)
    return x

_drawn_inputs = setup_inputs


def setup_inputs(seed=0):
    import zlib

    import numpy as np

    out = dict(_drawn_inputs(seed))
    spreads = {'L0_xattn_bq': (0.0, 0.417),
     'L0_xattn_bk': (0.0, 0.8),
     'L0_xattn_bv': (0.0, 0.1),
     'L0_xattn_bo': (0.0, 0.1),
     'L0_xattn_gamma': (1.0, 0.2),
     'L0_xattn_beta': (0.0, 0.1)}
    factors = {}
    for name, (base, spread) in spreads.items():
        noise = np.random.default_rng([zlib.crc32(name.encode()), seed]).standard_normal(out[name].shape)
        drawn = base * np.exp(spread * noise) if base else spread * noise
        out[name] = jnp.asarray(drawn.astype(out[name].dtype))
    for name, factor in factors.items():
        out[name] = (out[name] * factor).astype(out[name].dtype)
    return out
```

```python
from contextlib import ExitStack

import concourse.bass as bass
from concourse import mybir

ALU = mybir.AluOpType
ACT = mybir.ActivationFunctionType
AX = mybir.AxisListType
F32 = mybir.dt.float32
F32R = mybir.dt.float32r
F16 = mybir.dt.float16

P = 128
HEAD_DIM = 64
EPS = 1e-5
RMAX = bass.bass_isa.ReduceOp.max
C_RANGE = 2.0 ** 14
C_LEAST = 1e-30
UNROLL = 2


def cross_attention_kernel(nc, x, ctx_in, Wq, bq, Wk, bk, Wv, bv, Wo, bo, gamma, beta, out):
    B, QL, D = x.shape
    KL = ctx_in.shape[1]
    H = Wq.shape[1] // HEAD_DIM
    D_H = H * HEAD_DIM
    PAIRS = H // 2
    ROWS = H * QL
    KT = -(-KL // P)
    KTAIL = KL - (KT - 1) * P
    NBLK = -(-ROWS // P)
    ROW0 = [min(P * j, ROWS - P) for j in range(NBLK)]
    KEYCUT = [0, 480, 962, KL]
    TG = 4
    NT = KT // TG
    HG = 4
    NG = H // HG
    SLOTS = UNROLL * NBLK
    TURNS = B // UNROLL
    CT_AT = 0
    G_AT = CT_AT + NT
    FIN_AT = G_AT + NG
    NORM_AT = FIN_AT + 2
    CMAX_AT = 0
    CHI_AT = CMAX_AT + NT + 1
    with ExitStack() as es:
        def sb(name, shape, dt=F32):
            return es.enter_context(nc.sbuf_tensor(name, shape, dt))

        def sem(name):
            return es.enter_context(nc.semaphore(name))

        ident = sb("ident", [P, P])
        w_t = [sb(f"w_t{i}", [P, PAIRS, P]) for i in range(3)]
        wo_sb = sb("wo_sb", [P, PAIRS, P])
        bq_sb = sb("bq_sb", [P, PAIRS])
        bv_sb = sb("bv_sb", [P, PAIRS])
        rows_sb = sb("rows_sb", [1, 3, P])
        ones_row = sb("ones_row", [1, P])
        ones_pp = sb("ones_pp", [P, P])
        x_sb = sb("x_sb", [QL, B, D])
        xT = sb("xT", [P, B, QL])
        a_sb = sb("a_sb", [P, H, P])
        m_sb = sb("m_sb", [P, H, P])
        gb_sb = sb("gb_sb", [P, H])
        rows_b = sb("rows_b", [P, 3, P])
        c_raw = sb("c_raw", [P, 2, KT, D])
        c_hi = sb("c_hi", [P, 2, KT, D], F16)
        c_lo = sb("c_lo", [P, 2, KT, D], F16)
        c_max = sb("c_max", [P, 4])
        c_scaled = sb("c_scaled", [P, KT * D])
        c_top = sb("c_top", [P, 1])
        alpha = sb("alpha", [P, 2])
        unscale = sb("unscale", [P, 2])
        ct_raw = sb("ct_raw", [P, KT * P])
        ct_hi = sb("ct_hi", [P, 2, KL], F32R)
        ct_lo = sb("ct_lo", [P, 2, KL], F32R)
        g_raw = sb("g_raw", [P, H, QL])
        g_hi = sb("g_hi", [P, 2, ROWS], F32R)
        g_lo = sb("g_lo", [P, 2, ROWS], F32R)
        p32 = sb("p32", [P, 2, KT * P])
        pt_hi = sb("pt_hi", [P, 2, KT * P], F16)
        pt_lo = sb("pt_lo", [P, 2, KT * P], F16)
        pmax = sb("pmax", [P, 2, 3])
        nmax = sb("nmax", [P, 2])
        psums = sb("psums", [P, 2, 2])
        rsum = sb("rsum", [P, 2])
        rinv = sb("rinv", [P, 2])
        o_n = sb("o_n", [P, 2, D])
        o_t = sb("o_t", [P, 2, ROWS])
        w_all = o_t[:, :, :].rearrange("p a r -> p (a r)")
        w_raw = [w_all[:, i * D_H:(i + 1) * D_H] for i in range(3)]
        bv_wide = p32[:, 0, 0:PAIRS * P].rearrange("p (c m) -> p c m", m=P)
        z = sb("z", [QL, 2, D])
        stats = sb("stats", [QL, 2, 6])
        mv = sb("mv", [QL, 2, 2])
        vpe = sb("vpe", [QL, 2])
        rstd = sb("rstd", [QL, 2])
        mhalf = sb("mhalf", [QL, 1])
        zn = sb("zn", [QL, 2, D])
        zg = sb("zg", [QL, 2, D])
        y = sb("y", [QL, 2, D])

        ps = es.enter_context(nc.psum_tensor("ps", [P, 8, 512], F32))
        T0, O_BANK = 4, 7

        def s_bank(slot, k):
            return k if k else 3 * (slot % 2)

        s_w = [sem(f"w_loaded{i}") for i in range(3)]
        s_small = sem("small_loaded")
        s_x = sem("x_loaded")
        s_c = [sem(f"context_loaded{i}") for i in range(2)]
        s_const = sem("constants_set")
        s_id0 = sem("identity_zeroed")
        s_ident = sem("identity_ready")
        s_zero = sem("key_padding_zeroed")
        s_bvw = sem("bv_spread")
        s_part = sem("hi_part_ready")
        s_am = sem("context_group_max")
        s_cm = sem("context_partition_max")
        s_ca = sem("context_max")
        s_us = sem("unscale_ready")
        s_al = sem("alpha_ready")
        s_chi = sem("context_hi_ready")
        s_cs = sem("context_scaled")
        s_fill = sem("prologue_bank_filled")
        s_evd = sem("prologue_bank_emptied_by_vector")
        s_eva = sem("prologue_bank_emptied_by_scalar")
        s_xres = sem("residual_ready")
        s_rb = sem("bias_rows_ready")
        s_chl = sem("context_split")
        s_cts = sem("context_t_split")
        s_gs = sem("g_split")
        s_sc = sem("scores_ready")
        s_mx = sem("partial_max_ready")
        s_nm = sem("neg_max_ready")
        s_exp = sem("exp_ready")
        s_rs = sem("row_sum_ready")
        s_ri = sem("row_inverse_ready")
        s_tr = sem("p_transposed")
        s_hi = sem("p_hi_ready")
        s_lo = sem("p_lo_ready")
        s_pv = sem("pv_ready")
        s_on = sem("o_normalised")
        s_otr = sem("o_transposed")
        s_ot = sem("o_t_ready")
        s_ctj = sem("context_transposed")
        s_ctv = sem("context_t_copied")
        s_gj = sem("queries_projected")
        s_gv = sem("queries_copied")
        s_fin = sem("output_projected")
        s_z = sem("residual_added")
        s_st = sem("stats_ready")
        s_ag = sem("mean_var_ready")
        s_vp = sem("var_plus_eps_ready")
        s_rd = sem("rstd_ready")
        s_zn = sem("normed_ready")
        s_zg = sem("gamma_applied")
        s_y = sem("y_ready")
        s_out = [sem(f"stored{i}") for i in range(2)]
        s_idle = sem("waited_apart")

        N_W, N_X = 6, B // 4
        J_X = N_W
        J_A = J_X + N_X
        J_M = J_A + NG
        J_R = J_M + NG
        J_C = J_R + 2
        J_G = J_C + NT
        N_PRO = J_G + NG
        N_SMALL = 6
        SCALE = float(HEAD_DIM) ** -0.5

        def every_other(g):
            first = g // 2 * 2 * HG + g % 2
            return slice(first, first + 2 * HG - 1, 2)

        def context_landed(b, par):
            return 32 * (b // UNROLL + 1) if isinstance(b, int) else 16 * (b - par) + 32

        def emptied(eng, k):
            eng.wait_ge(s_evd if k % 2 == 0 else s_eva, k // 2 + 1)

        def wait_apart(eng, counter, value):
            eng.wait_ge(counter, value)
            if not isinstance(value, int):
                eng.sem_inc(s_idle, 1)

        block = es.enter_context(nc.Block())

        def turns(eng, step):
            step(0, True, False)
            with eng.Fori(1, TURNS - 1) as t:
                step(t, False, False)
            step(TURNS - 1, False, True)

        @block.sync
        def _(sp):
            def load_context(b, par):
                whole = ctx_in[bass.ds(b, 1), 0:(KT - 1) * P, :].rearrange("o (t p) d -> p (o t) d", p=P)
                tail = ctx_in[bass.ds(b, 1), (KT - 1) * P:KL, :].rearrange("o p d -> p o d")
                sp.dma_start(c_raw[:, par, 0:KT - 1, :], whole).then_inc(s_c[par], 16)
                sp.dma_start(c_raw[0:KTAIL, par, KT - 1:KT, :], tail).then_inc(s_c[par], 16)

            sp.sem_inc(s_out[1], 16)
            for i, w in enumerate((Wq, Wk, Wv)):
                sp.dma_start(w_raw[i][:, :], w).then_inc(s_w[i], 16)
            sp.dma_start(x_sb[:, :, :], x.rearrange("b q d -> q b d")).then_inc(s_x, 16)
            sp.dma_start(wo_sb[:, :, :], Wo.rearrange("(c p) o -> p c o", p=P)).then_inc(s_small, 16)
            sp.wait_ge(s_zero, 1)
            for b in range(UNROLL):
                load_context(b, b)

            def step(t, first, last):
                for u in range(UNROLL):
                    b = t * UNROLL + u
                    b_next, b_done = (b + UNROLL, b - 1) if first or last else (sp.snap(b + UNROLL), sp.snap(b - 1))
                    if not last:
                        wait_apart(sp, s_chl, b + 1)
                        if first and u == 0:
                            sp.wait_ge(s_fill, J_C + NT)
                        else:
                            wait_apart(sp, s_ctj, NT * b)
                        load_context(b_next, u)
                    if not (first and u == 0):
                        wait_apart(sp, s_y, b + 1)
                        sp.dma_start(out[bass.ds(b_done, 1), :, :].rearrange("o q d -> q o d"),
                                     y[:, (u + 1) % 2:(u + 1) % 2 + 1, :]).then_inc(s_out[(u + 1) % 2], 16)

            turns(sp, step)
            sp.wait_ge(s_y, B + 1)
            sp.dma_start(out[B - 1, :, :], y[:, (B - 1) % 2, :]).then_inc(s_out[(B - 1) % 2], 16)
            sp.wait_ge(s_out[0], 16 * TURNS)
            sp.wait_ge(s_out[1], 16 * (TURNS + 1))

        @block.tensor
        def _(pe):
            def take(k):
                if k >= 4:
                    emptied(pe, k - 4)
                return ps[:, k % 4, :]

            def half_rows(h):
                return slice(HEAD_DIM * (h % 2), HEAD_DIM * (h % 2) + HEAD_DIM)

            def transpose_context(bank, par, g):
                for c in range(TG):
                    mm = pe.transpose(bank[:, c * P:(c + 1) * P], c_raw[:, par, TG * g + c, :], ident[:, :])
                return mm

            def project_queries(bank, b, g):
                for c in range(HG):
                    mm = pe.matmul(bank[:, c * QL:(c + 1) * QL], a_sb[:, HG * g + c, :],
                                   xT[:, bass.ds(b, 1), :].rearrange("p o q -> p (o q)"), start=True, stop=True)
                return mm

            def project_out(bank, par):
                for h in range(H):
                    mm = pe.matmul(bank[0:QL, 0:P], o_t[:, par, h * QL:(h + 1) * QL], m_sb[:, h, :],
                                   start=(h == 0), stop=(h == H - 1))
                return mm

            pe.wait_ge(s_ident, 1)
            pe.wait_ge(s_const, 1)
            for i in range(3):
                pe.wait_ge(s_w[i], 16)
                for half in range(2):
                    bank = take(2 * i + half)
                    for c in range(4):
                        col = (4 * half + c) * P
                        mm = pe.transpose(bank[:, c * P:(c + 1) * P], w_raw[i][:, col:col + P], ident[:, :])
                    mm.then_inc(s_fill, 1)
            pe.wait_ge(s_x, 16)
            for g in range(N_X):
                bank = take(J_X + g)
                for c in range(4):
                    mm = pe.transpose(bank[:, c * QL:(c + 1) * QL], x_sb[:, 4 * g + c, :], ident[0:QL, 0:QL])
                mm.then_inc(s_fill, 1)
            pe.wait_ge(s_small, 16 * N_SMALL)
            for k in range(N_W - 2, N_W):
                emptied(pe, k)
            for lhs, rhs, j0 in ((w_t[0], w_t[1], J_A), (w_t[2], wo_sb, J_M)):
                for g in range(NG):
                    bank = take(j0 + g)
                    for c, h in enumerate(range(H)[every_other(g)]):
                        mm = pe.matmul(bank[:, c * P:(c + 1) * P], lhs[half_rows(h), h // 2, :],
                                       rhs[half_rows(h), h // 2, :], start=True, stop=True)
                    mm.then_inc(s_fill, 1)
            def bias_columns(bank, odd):
                for c in range(PAIRS):
                    mm = pe.matmul(bank[:, c:c + 1], w_t[1][half_rows(odd), c, :], bq_sb[half_rows(odd), c:c + 1],
                                   start=True, stop=True)
                return mm

            bias_columns(take(J_R), 0).then_inc(s_fill, 1)
            bank = take(J_R + 1)
            pe.wait_ge(s_bvw, 1)
            for c in range(PAIRS):
                pe.matmul(bank[:, 0:P], bv_wide[:, c, :], wo_sb[:, c, :], start=(c == 0), stop=False)
            pe.matmul(bank[:, 0:P], ones_row[:, :], rows_sb[:, 0, :], start=False, stop=True)
            pe.matmul(bank[:, P:2 * P], ones_row[:, :], rows_sb[:, 1, :], start=True, stop=True)
            pe.matmul(bank[:, 2 * P:3 * P], ones_row[:, :], rows_sb[:, 2, :], start=True, stop=True)
            bias_columns(bank[:, 3 * P:3 * P + PAIRS], 1).then_inc(s_fill, 1)
            pe.wait_ge(s_c[0], 32)
            for g in range(NT):
                transpose_context(take(J_C + g), 0, g).then_inc(s_fill, 1)
            for g in range(NG):
                project_queries(take(J_G + g), 0, g).then_inc(s_fill, 1)

            def scores(n, slot, before, between=None):
                par, row = slot // NBLK, ROW0[slot % NBLK]
                gh, gl = g_hi[:, par, row:row + P], g_lo[:, par, row:row + P]
                for k in range(3):
                    if k == 0 and before == 2:
                        pe.wait_ge(s_exp, 2 * n - 2)
                    if k == 1 and between:
                        between()
                    if k == 1 and before >= 1:
                        pe.wait_ge(s_exp, 2 * n - 1)
                    a, e = KEYCUT[k], KEYCUT[k + 1]
                    o = ps[:, s_bank(slot, k), 0:e - a]
                    pe.matmul(o, gh, ct_hi[:, par, a:e], start=True, stop=False)
                    pe.matmul(o, gh, ct_lo[:, par, a:e], start=False, stop=False)
                    pe.matmul(o, gl, ct_hi[:, par, a:e], start=False, stop=True).then_inc(s_sc, 1)

            def weigh(n, slot, b, is_first):
                if not is_first:
                    pe.wait_ge(s_ot, n)
                if slot % NBLK == 0:
                    pe.wait_ge(s_chl, b + 1)
                o = ps[:, O_BANK, 0:D]
                for i in range(KT):
                    if i % TG == 0:
                        pe.wait_ge(s_lo, NT * n + i // TG + 1)
                    ph = pt_hi[:, slot % 2, i * P:(i + 1) * P]
                    pl = pt_lo[:, slot % 2, i * P:(i + 1) * P]
                    pe.matmul(o, ph, c_hi[:, slot // NBLK, i, :], start=(i == 0), stop=False)
                    pe.matmul(o, ph, c_lo[:, slot // NBLK, i, :], start=False, stop=False)
                    mm = pe.matmul(o, pl, c_hi[:, slot // NBLK, i, :], start=False, stop=(i == KT - 1))
                mm.then_inc(s_pv, 1)

            def turn_result(n, slot):
                pe.wait_ge(s_on, n + 1)
                pe.transpose(ps[:, O_BANK, 256:256 + P], o_n[:, slot % 2, :], ident[:, :]).then_inc(s_otr, 1)

            def step(t, first, last):
                for slot in range(SLOTS):
                    n, j, u = t * SLOTS + slot, slot % NBLK, slot // NBLK
                    b = t * UNROLL + u
                    start, ahead = first and slot == 0, not (last and u == UNROLL - 1)
                    if not (last and slot == SLOTS - 1):
                        if j == NBLK - 1:
                            pe.wait_ge(s_cts, b + 2)
                            pe.wait_ge(s_gs, b + 2)
                        scores(n + 1, (slot + 1) % SLOTS, 1 if start else 2,
                               None if first and slot < 2 else lambda: turn_result(n - 2, (slot - 2) % SLOTS))
                    else:
                        turn_result(n - 2, (slot - 2) % SLOTS)
                    pe.wait_ge(s_exp, 2 * n + 2)
                    if CT_AT < j <= G_AT and ahead:
                        pe.wait_ge(s_ctv, NT * b + j - CT_AT)
                    if G_AT < j <= FIN_AT and ahead:
                        pe.wait_ge(s_gv, NG * b + j - G_AT)
                    if j == FIN_AT + 1 and not (first and u == 0):
                        pe.wait_ge(s_z, b)
                    for k in range(NT):
                        if not start:
                            pe.wait_ge(s_lo, NT * n - NT + k + 1)
                        for c in range(TG):
                            col = (TG * k + c) * P
                            mm = pe.transpose(ps[:, T0 + k, c * P:(c + 1) * P], p32[:, slot % 2, col:col + P],
                                              ident[:, :])
                        mm.then_inc(s_tr, 1)
                    if not start:
                        weigh(n - 1, (slot - 1) % SLOTS, b if j else b - 1, first and slot == 1)
                    bank = ps[:, T0, :]
                    if CT_AT <= j < FIN_AT and ahead or j == FIN_AT and not (first and u == 0):
                        pe.wait_ge(s_lo, NT * n + 1)
                    if CT_AT <= j < G_AT and ahead:
                        if j == CT_AT:
                            pe.wait_ge(s_c[(u + 1) % 2], 32 * (t + 1 + u))
                        transpose_context(bank, (u + 1) % 2, j - CT_AT).then_inc(s_ctj, 1)
                    elif G_AT <= j < FIN_AT and ahead:
                        project_queries(bank, b + 1, j - G_AT).then_inc(s_gj, 1)
                    elif j == FIN_AT and not (first and u == 0):
                        pe.wait_ge(s_ot, NBLK * b)
                        project_out(bank, (u + 1) % 2).then_inc(s_fin, 1)

            for k in range(N_PRO - 4, N_PRO):
                emptied(pe, k)
            pe.wait_ge(s_cts, 1)
            pe.wait_ge(s_gs, 1)
            scores(0, 0, 0)
            turns(pe, step)
            last_n = B * NBLK - 1
            turn_result(last_n - 1, SLOTS - 2)
            weigh(last_n, SLOTS - 1, B - 1, False)
            turn_result(last_n, SLOTS - 1)
            pe.wait_ge(s_ot, NBLK * B)
            project_out(ps[:, T0, :], (B - 1) % 2).then_inc(s_fin, 1)

        def empty_prologue(eng, parity, s_done, copy, scale, add_bias):
            for k in range(parity, N_PRO, 2):
                eng.wait_ge(s_fill, k + 1)
                bank = ps[:, k % 4, :]
                if k < J_X:
                    last = copy(w_t[k // 2][:, 4 * (k % 2):4 * (k % 2) + 4, :], split(bank, 4, P))
                elif k < J_A:
                    g = k - J_X
                    last = copy(xT[:, 4 * g:4 * g + 4, :], split(bank, 4, QL))
                elif k < J_M:
                    g = k - J_A
                    last = scale(a_sb[:, every_other(g), :], split(bank, HG, P))
                elif k < J_R:
                    g = k - J_M
                    last = copy(m_sb[:, every_other(g), :], split(bank, HG, P))
                elif k == J_R:
                    last = scale(gb_sb[:, 0:H:2], bank[:, 0:PAIRS])
                elif k == J_R + 1:
                    copy(rows_b[:, :, :], split(bank, 3, P))
                    last = scale(gb_sb[:, 1:H:2], bank[:, 3 * P:3 * P + PAIRS])
                elif k < J_G:
                    g = k - J_C
                    last = copy(ct_raw[:, TG * P * g:TG * P * (g + 1)], bank)
                else:
                    emptied(eng, J_R)
                    emptied(eng, J_R + 1)
                    last = add_bias(k - J_G, bank)
                last.then_inc(s_done, 1)

        def split(bank, n, w):
            return bank[:, 0:n * w].rearrange("p (n w) -> p n w", w=w)

        @block.vector
        def _(dve):
            def add_bias(g, bank):
                heads = slice(HG * g, HG * g + HG)
                return dve.tensor_tensor(g_raw[:, heads, :], split(bank, HG, QL),
                                         gb_sb[:, heads].unsqueeze(2).to_broadcast([P, HG, QL]), ALU.add)

            dve.memset(ones_row[:, :], 1.0)
            dve.memset(mhalf[:, :], -0.5)
            dve.memset(p32[:, :, KL:KT * P], 0.0).then_inc(s_const, 1)
            dve.wait_ge(s_small, 16 * N_SMALL)
            dve.tensor_copy(bv_wide[:, :, :], bv_sb[:, :].unsqueeze(2).to_broadcast([P, PAIRS, P])).then_inc(s_bvw, 1)
            empty_prologue(dve, 0, s_evd, dve.tensor_copy,
                           lambda o, i: dve.tensor_scalar(o, i, SCALE, None, ALU.mult), add_bias)

            def row_max(n, slot):
                par = slot % 2
                for k in range(3):
                    dve.wait_ge(s_sc, 3 * n + k + 1)
                    dve.tensor_reduce(pmax[:, par, k:k + 1], ps[:, s_bank(slot, k), 0:KEYCUT[k + 1] - KEYCUT[k]],
                                      AX.X, ALU.max).then_inc(s_mx, 1)
                dve.wait_ge(s_mx, 3 * n + 3)
                dve.tensor_reduce(nmax[:, par:par + 1], pmax[:, par, :], AX.X, ALU.max, negate=True).then_inc(s_nm, 1)

            def lo_part(n, slot, k):
                cols = slice(TG * P * k, TG * P * (k + 1))
                dve.wait_ge(s_hi, NT * n + k + 1)
                dve.tensor_tensor(pt_lo[:, slot % 2, cols], ps[:, T0 + k, :], pt_hi[:, slot % 2, cols],
                                  ALU.subtract).then_inc(s_lo, 1)

            def row_sum(n, slot):
                dve.wait_ge(s_exp, 2 * n + 2)
                dve.tensor_tensor(rsum[:, slot % 2:slot % 2 + 1], psums[:, slot % 2, 0:1], psums[:, slot % 2, 1:2],
                                  ALU.add).then_inc(s_rs, 1)

            def row_inverse(n, slot):
                dve.wait_ge(s_rs, n + 1)
                dve.reciprocal(rinv[:, slot % 2:slot % 2 + 1], rsum[:, slot % 2:slot % 2 + 1]).then_inc(s_ri, 1)

            def normalise(n, slot):
                dve.wait_ge(s_ri, n + 1)
                dve.wait_ge(s_pv, n + 1)
                par = slot // NBLK
                dve.tensor_scalar(o_n[:, slot % 2, :], ps[:, O_BANK, 0:D], rinv[:, slot % 2:slot % 2 + 1],
                                  unscale[:, par:par + 1], ALU.mult, ALU.mult).then_inc(s_on, 1)

            def context_max(b, par, g):
                if g == 0:
                    dve.wait_ge(s_c[par], context_landed(b, par))
                dve.tensor_reduce(c_max[:, g:g + 1], c_raw[:, par, TG * g:TG * g + TG, :].rearrange("p t d -> p (t d)"),
                                  AX.X, ALU.max, apply_absolute_value=True).then_inc(s_am, 1)
                if g == NT - 1:
                    dve.wait_ge(s_am, NT * b + NT)
                    dve.tensor_reduce(c_max[:, NT:NT + 1], c_max[:, 0:NT], AX.X, ALU.max).then_inc(s_cm, 1)

            def context_scale(b, par):
                dve.wait_ge(s_ca, b + 1)
                dve.tensor_scalar(unscale[:, par:par + 1], c_top[:, :], C_LEAST, 1.0 / C_RANGE, ALU.max,
                                  ALU.mult).then_inc(s_us, 1)
                dve.wait_ge(s_us, b + 1)
                dve.reciprocal(alpha[:, par:par + 1], unscale[:, par:par + 1]).then_inc(s_al, 1)

            def take_context(b, g):
                dve.wait_ge(s_ctj, NT * (b - 1) + g + 1)
                if g == 0:
                    dve.wait_ge(s_cts, b)
                dve.tensor_copy(ct_raw[:, TG * P * g:TG * P * (g + 1)], ps[:, T0, :]).then_inc(s_ctv, 1)

            def take_queries(b, g):
                dve.wait_ge(s_gj, NG * (b - 1) + g + 1)
                if g == 0:
                    dve.wait_ge(s_gs, b)
                add_bias(g, ps[:, T0, :]).then_inc(s_gv, 1)

            def take_rows(b, par, has_older):
                dve.wait_ge(s_fin, b + 1)
                if has_older:
                    dve.wait_ge(s_y, b)
                dve.tensor_tensor(z[:, par:par + 1, :], ps[0:QL, T0, 0:D].unsqueeze(1), x_sb[:, bass.ds(b, 1), :],
                                  ALU.add).then_inc(s_z, 1)
                dve.wait_ge(s_z, b + 1)
                dve.bn_stats(stats[:, par, :], z[:, par, :]).then_inc(s_st, 1)
                wait_apart(dve, s_st, b + 1)
                dve.bn_aggr(mv[:, par, :], stats[:, par, :]).then_inc(s_ag, 1)

            def norm_rows(b, par):
                dve.wait_ge(s_rd, b + 1)
                dve.tensor_scalar(zn[:, par, :], z[:, par, :], mv[:, par, 0:1], rstd[:, par:par + 1], ALU.subtract,
                                  ALU.mult).then_inc(s_zn, 1)

            def step(t, first, last):
                for slot in range(SLOTS):
                    n, j, u = t * SLOTS + slot, slot % NBLK, slot // NBLK
                    b = t * UNROLL + u
                    ahead = not (last and u == UNROLL - 1)
                    if not (last and slot == SLOTS - 1):
                        row_max(n + 1, (slot + 1) % SLOTS)
                    lo_part(n, slot, 0)
                    row_sum(n, slot)
                    lo_part(n, slot, 1)
                    row_inverse(n, slot)
                    lo_part(n, slot, 2)
                    if not (first and slot == 0):
                        normalise(n - 1, (slot - 1) % SLOTS)
                    if CMAX_AT <= j < CMAX_AT + NT and ahead:
                        context_max(b + 1, (u + 1) % 2, j - CMAX_AT)
                    elif j == CMAX_AT + NT and ahead:
                        context_scale(b + 1, (u + 1) % 2)
                    if CT_AT <= j < G_AT and ahead:
                        take_context(b + 1, j - CT_AT)
                    elif G_AT <= j < FIN_AT and ahead:
                        take_queries(b + 1, j - G_AT)
                    elif j == FIN_AT and not (first and u == 0):
                        take_rows(b - 1, (u + 1) % 2, not first)
                    elif j == NORM_AT and not (first and u == 0):
                        norm_rows(b - 1, (u + 1) % 2)

            for g in range(NT):
                context_max(0, 0, g)
            context_scale(0, 0)
            row_max(0, 0)
            turns(dve, step)
            normalise(B * NBLK - 1, SLOTS - 1)
            take_rows(B - 1, (B - 1) % 2, True)
            norm_rows(B - 1, (B - 1) % 2)

        @block.scalar
        def _(act):
            act.dma_start(bq_sb[:, :], bq.rearrange("(c p) -> p c", p=P), allow_slow_non_contiguous=True).then_inc(s_small, 16)
            act.dma_start(bv_sb[:, :], bv.rearrange("(c p) -> p c", p=P), allow_slow_non_contiguous=True).then_inc(s_small, 16)
            for i, r in enumerate((bo, gamma, beta)):
                act.dma_start(rows_sb[:, i, :], r.rearrange("(o d) -> o d", o=1)).then_inc(s_small, 16)

            def add_bias(g, bank):
                for c in range(HG):
                    h = HG * g + c
                    last = act.activation(g_raw[:, h, :], bank[:, c * QL:(c + 1) * QL], ACT.Identity,
                                          bias=gb_sb[:, h:h + 1])
                return last

            empty_prologue(act, 1, s_eva, act.copy, lambda o, i: act.mul(o, i, SCALE), add_bias)

            def exponentials(n, slot, has_older):
                par = slot % 2
                act.wait_ge(s_nm, n + 1)
                if has_older:
                    act.wait_ge(s_rs, n - 1)
                    act.wait_ge(s_tr, NT * (n - 1))
                w = KEYCUT[2] - KEYCUT[1]
                act.activation(p32[:, par, KEYCUT[1]:KEYCUT[3]].rearrange("p (k w) -> p k w", w=w), ps[:, 1:3, 0:w],
                               ACT.Exp, bias=nmax[:, par:par + 1], accum_out=psums[:, par, 0:1]).then_inc(s_exp, 1)
                act.activation(p32[:, par, 0:KEYCUT[1]], ps[:, s_bank(slot, 0), 0:KEYCUT[1]], ACT.Exp,
                               bias=nmax[:, par:par + 1], accum_out=psums[:, par, 1:2]).then_inc(s_exp, 1)

            def hi_part(n, slot, k, has_older):
                if has_older and k == 0:
                    act.wait_ge(s_pv, n - 1)
                act.wait_ge(s_tr, NT * n + k + 1)
                cols = slice(TG * P * k, TG * P * (k + 1))
                act.copy(pt_hi[:, slot % 2, cols], ps[:, T0 + k, :]).then_inc(s_hi, 1)

            def context_hi(b, par, g):
                if g == 0:
                    act.wait_ge(s_al, b + 1)
                tiles = slice(TG * g, TG * g + TG)
                act.activation(c_hi[:, par, tiles, :].rearrange("p t d -> p (t d)"),
                               c_raw[:, par, tiles, :].rearrange("p t d -> p (t d)"), ACT.Copy,
                               scale=alpha[:, par:par + 1]).then_inc(s_chi, 1)

            def take_result(n, slot, b, has_older):
                act.wait_ge(s_otr, n + 1)
                j = slot % NBLK
                if j == 0 and has_older:
                    act.wait_ge(s_fin, b - 1)
                act.copy(o_t[:, slot // NBLK, ROW0[j]:ROW0[j] + P], ps[:, O_BANK, 256:256 + P]).then_inc(s_ot, 1)

            def step(t, first, last):
                for slot in range(SLOTS):
                    n = t * SLOTS + slot
                    if not (first and slot < 2):
                        s2 = (slot - 2) % SLOTS
                        b2 = t * UNROLL + slot // NBLK if slot % NBLK >= 2 else t * UNROLL + slot // NBLK - 1
                        take_result(n - 2, s2, b2, not first)
                    for k in range(NT):
                        hi_part(n, slot, k, not (first and slot < 2))
                    j, u = slot % NBLK, slot // NBLK
                    if CHI_AT <= j < CHI_AT + NT and not (last and u == UNROLL - 1):
                        context_hi(t * UNROLL + u + 1, (u + 1) % 2, j - CHI_AT)
                    if not (last and slot == SLOTS - 1):
                        exponentials(n + 1, (slot + 1) % SLOTS, not (first and slot == 0))

            for g in range(NT):
                context_hi(0, 0, g)
            exponentials(0, 0, False)
            turns(act, step)
            for slot in (SLOTS - 2, SLOTS - 1):
                take_result(B * NBLK - SLOTS + slot, slot, B - 1, True)

        @block.gpsimd
        def _(pool):
            pool.sem_inc(s_y, 1)
            pool.memset(ident[:, :], 0.0).then_inc(s_id0, 1)
            pool.wait_ge(s_id0, 1)
            pool.affine_select(out=ident[:, :], in_=ident[:, :], compare_op=ALU.not_equal, fill=1.0, base=0,
                               pattern=[[-1, P]], channel_multiplier=1).then_inc(s_ident, 1)
            pool.memset(c_raw[:, :, KT - 1, :], 0.0).then_inc(s_zero, 1)

            PARTS = NT + NG

            def split_parts(hi, lo, raw, count, s_done):
                pool.tensor_copy(hi, raw).then_inc(s_part, 1)
                wait_apart(pool, s_part, count)
                done = pool.tensor_tensor(lo, raw, hi.bitcast(F32), ALU.subtract)
                if s_done is not None:
                    done.then_inc(s_done, 1)

            def context_top(b):
                wait_apart(pool, s_cm, b + 1)
                pool.partition_all_reduce(c_top[:, :], c_max[:, NT:NT + 1], P, RMAX).then_inc(s_ca, 1)

            def context_lo(b, par):
                wait_apart(pool, s_chi, NT * b + NT)
                flat = "p t d -> p (t d)"
                pool.tensor_scalar(c_scaled[:, :], c_raw[:, par, :, :].rearrange(flat), alpha[:, par:par + 1], 1.0,
                                   ALU.mult, ALU.mult).then_inc(s_cs, 1)
                wait_apart(pool, s_cs, b + 1)
                pool.tensor_tensor(c_lo[:, par, :, :].rearrange(flat), c_scaled[:, :],
                                   c_hi[:, par, :, :].rearrange(flat), ALU.subtract).then_inc(s_chl, 1)

            def split_context_t(b, par, g):
                cols = slice(TG * P * g, min(TG * P * (g + 1), KL))
                split_parts(ct_hi[:, par, cols], ct_lo[:, par, cols], ct_raw[:, cols], PARTS * b + 1 + g,
                            s_cts if g == NT - 1 else None)

            def split_queries(b, par, g):
                cols = slice(HG * QL * g, HG * QL * (g + 1))
                split_parts(g_hi[:, par, cols], g_lo[:, par, cols],
                            g_raw[:, HG * g:HG * g + HG, :].rearrange("p h q -> p (h q)"), PARTS * b + 1 + NT + g,
                            s_gs if g == NG - 1 else None)

            def inverse_deviation(b, par):
                wait_apart(pool, s_ag, b + 1)
                pool.tensor_scalar(vpe[:, par:par + 1], mv[:, par, 1:2], EPS, None, ALU.add).then_inc(s_vp, 1)
                wait_apart(pool, s_vp, b + 1)
                pool.tensor_tensor(rstd[:, par:par + 1], vpe[:, par:par + 1], mhalf[:, :], ALU.pow).then_inc(s_rd, 1)

            def scale_rows(b, par, counted):
                wait_apart(pool, s_zn, b + 1)
                pool.tensor_tensor(zg[:, par, :], zn[:, par, :], rows_b[0:QL, 1, :], ALU.mult).then_inc(s_zg, 1)
                wait_apart(pool, s_zg, b + 1)
                if not isinstance(counted, int) or counted > 0:
                    wait_apart(pool, s_out[par], 16 * counted)
                pool.tensor_tensor(y[:, par, :], zg[:, par, :], rows_b[0:QL, 2, :], ALU.add).then_inc(s_y, 1)

            context_top(0)
            context_lo(0, 0)
            emptied(pool, J_R + 1)
            pool.wait_ge(s_fill, J_A)
            pool.tensor_tensor(x_sb[:, :, :], x_sb[:, :, :], rows_b[0:QL, 0:1, :].to_broadcast([QL, B, D]),
                               ALU.add).then_inc(s_xres, 1)
            for g in range(NT):
                emptied(pool, J_C + g)
                split_context_t(0, 0, g)
            for g in range(NG):
                emptied(pool, J_G + g)
                split_queries(0, 0, g)

            def step(t, first, last):
                for u in range(UNROLL):
                    b, other = t * UNROLL + u, (u + 1) % 2
                    if not (last and u == UNROLL - 1):
                        for g in range(NT):
                            wait_apart(pool, s_ctv, NT * b + g + 1)
                            split_context_t(b + 1, other, g)
                        context_top(b + 1)
                        context_lo(b + 1, other)
                        for g in range(NG):
                            wait_apart(pool, s_gv, NG * b + g + 1)
                            split_queries(b + 1, other, g)
                    if not (first and u == 0):
                        inverse_deviation(b - 1, other)
                        scale_rows(b - 1, other, t)

            turns(pool, step)
            inverse_deviation(B - 1, (B - 1) % 2)
            scale_rows(B - 1, (B - 1) % 2, TURNS)


_INS = ['x', 'ctx_1024', 'L0_xattn_Wq', 'L0_xattn_bq', 'L0_xattn_Wk', 'L0_xattn_bk', 'L0_xattn_Wv', 'L0_xattn_bv',
        'L0_xattn_Wo', 'L0_xattn_bo', 'L0_xattn_gamma', 'L0_xattn_beta']
_OUTS = [((16, 100, 128), 'float32')]


def kernel(**inputs):
    import numpy as _np
    import concourse.bacc as _bacc
    from concourse import mybir as _mybir
    from concourse.bass_utils import run_bass_kernel_spmd as _run

    nc = _bacc.Bacc("TRN2", target_bir_lowering=False, num_devices=1)
    arrays, args = {}, []
    for name in _INS:
        a = _np.ascontiguousarray(inputs[name])
        arrays[f"in_{name}_dram"] = a
        args.append(nc.dram_tensor(f"in_{name}_dram", a.shape, _mybir.dt.from_np(a.dtype), kind="ExternalInput").ap())
    for i, (shape, dtype) in enumerate(_OUTS):
        dt = _mybir.dt.from_np(_np.dtype(dtype))
        args.append(nc.dram_tensor(f"out_{i}_dram", shape, dt, kind="ExternalOutput").ap())
    cross_attention_kernel(nc, *args)
    r = _run(nc, [arrays], core_ids=[0])
    got = tuple(r.results[0][f"out_{i}_dram"] for i in range(len(_OUTS)))
    return got[0]
```

```python
from contextlib import ExitStack

import concourse.bass as bass
from concourse import mybir

ALU = mybir.AluOpType
ACT = mybir.ActivationFunctionType
AX = mybir.AxisListType
F32 = mybir.dt.float32
F32R = mybir.dt.float32r
F16 = mybir.dt.float16

P = 128
HEAD_DIM = 64
EPS = 1e-5
RMAX = bass.bass_isa.ReduceOp.max
C_RANGE = 2.0 ** 14
P_RANGE = 2.0 ** 14
C_LEAST = 1e-30
UNROLL = 2


def cross_attention_kernel(nc, x, ctx_in, Wq, bq, Wk, bk, Wv, bv, Wo, bo, gamma, beta, out):
    B, QL, D = x.shape
    KL = ctx_in.shape[1]
    H = Wq.shape[1] // HEAD_DIM
    D_H = H * HEAD_DIM
    PAIRS = H // 2
    ROWS = H * QL
    KT = -(-KL // P)
    KTAIL = KL - (KT - 1) * P
    NBLK = -(-ROWS // P)
    ROW0 = [min(P * j, ROWS - P) for j in range(NBLK)]
    NEW_ROWS = [P] * (NBLK - 1) + [ROWS - P * (NBLK - 1)]
    KEYW = 482
    KEYCUT = [0, KEYW, KL - KEYW]
    TWICE = 3 * KEYW - KL
    LAG = 4
    TG = 4
    NT = KT // TG
    HG = 4
    NG = H // HG
    SLOTS = UNROLL * NBLK
    TURNS = B // UNROLL
    CT_AT = 0
    FIN_AT = LAG
    G_AT = FIN_AT + NG
    ROWS_AT = G_AT
    NORM_AT = ROWS_AT + 2
    CMAX_AT = 1
    SCALE_AT = CMAX_AT + NT + 1
    CHI_AT = SCALE_AT + 1
    LOAD_AT = 2
    STORE_AT = NBLK - 1
    with ExitStack() as es:
        def sb(name, shape, dt=F32):
            return es.enter_context(nc.sbuf_tensor(name, shape, dt))

        def sem(name):
            return es.enter_context(nc.semaphore(name))

        ident = sb("ident", [P, P])
        w_t = [sb(f"w_t{i}", [P, PAIRS, P]) for i in range(3)]
        wo_sb = sb("wo_sb", [P, PAIRS, P])
        bq_sb = sb("bq_sb", [P, PAIRS])
        bv_sb = sb("bv_sb", [P, PAIRS])
        bv_wide = sb("bv_wide", [P, PAIRS, P])
        rows_sb = sb("rows_sb", [1, 3, P])
        ones_row = sb("ones_row", [1, P])
        ones_pp = sb("ones_pp", [P, P])
        x_sb = sb("x_sb", [QL, B, D])
        xT = sb("xT", [P, B, QL])
        a_sb = sb("a_sb", [P, H, P])
        m_sb = sb("m_sb", [P, H, P])
        gb_sb = sb("gb_sb", [P, H])
        rows_b = sb("rows_b", [P, 3, P])
        c_raw = sb("c_raw", [P, 2, KT, D])
        c_hl = sb("c_hl", [P, 2, KT, 2 * D], F16)
        c_max = sb("c_max", [P, 4])
        c_scaled = sb("c_scaled", [P, KT * D])
        c_top = sb("c_top", [P, 1])
        alpha = sb("alpha", [P, 2])
        unscale = sb("unscale", [P, 2])
        ct_hi = sb("ct_hi", [P, 2, KL], F32R)
        ct_lo = sb("ct_lo", [P, 2, KL], F32R)
        g_raw = sb("g_raw", [P, H, QL])
        g_hi = sb("g_hi", [P, 2, ROWS], F32R)
        g_lo = sb("g_lo", [P, 2, ROWS], F32R)
        p32 = sb("p32", [P, 4, KL])
        p_hi = sb("p_hi", [P, 2, KT * P], F16)
        p_lo = sb("p_lo", [P, 2, KT * P], F16)
        pt_hi = sb("pt_hi", [P, 2, KT, P], F16)
        pt_lo = sb("pt_lo", [P, 2, KT, P], F16)
        nmax = sb("nmax", [P, SLOTS])
        psums = sb("psums", [P, SLOTS, 2])
        rsum = sb("rsum", [P, SLOTS])
        rinv = sb("rinv", [P, SLOTS])
        o_t = sb("o_t", [P, 2, ROWS])
        w_all = o_t[:, :, :].rearrange("p a r -> p (a r)")
        w_raw = [w_all[:, i * D_H:(i + 1) * D_H] for i in range(3)]
        z = sb("z", [QL, 2, D])
        stats = sb("stats", [QL, 2, 6])
        mv = sb("mv", [QL, 2, 2])
        vpe = sb("vpe", [QL, 2])
        rstd = sb("rstd", [QL, 2])
        mhalf = sb("mhalf", [QL, 1])
        zn = sb("zn", [QL, 2, D])
        zg = sb("zg", [QL, 2, D])
        y = sb("y", [QL, 2, D])

        ps = es.enter_context(nc.psum_tensor("ps", [P, 8, 512], F32))
        O_BANK, JOB_BANK = 6, 7

        s_w = [sem(f"w_loaded{i}") for i in range(3)]
        s_small = sem("small_loaded")
        s_x = [sem(f"x_loaded{i}") for i in range(2)]
        s_c = [sem(f"context_loaded{i}") for i in range(2)]
        s_const = sem("constants_set")
        s_id0 = sem("identity_zeroed")
        s_ident = sem("identity_ready")
        s_zero = sem("key_padding_zeroed")
        s_bvw = sem("bv_spread")
        s_part = sem("hi_part_ready")
        s_am = sem("context_group_max")
        s_cm = sem("context_partition_max")
        s_ca = sem("context_max")
        s_us = sem("unscale_ready")
        s_al = sem("alpha_ready")
        s_chi = sem("context_hi_ready")
        s_cs = sem("context_scaled")
        s_fill = sem("prologue_bank_filled")
        s_evd = sem("prologue_bank_emptied_by_vector")
        s_eva = sem("prologue_bank_emptied_by_scalar")
        s_xres = sem("residual_ready")
        s_rb = sem("bias_rows_ready")
        s_chl = sem("context_split")
        s_cth = sem("context_t_hi_ready")
        s_cts = sem("context_t_split")
        s_gs = sem("g_split")
        s_sc = sem("scores_ready")
        s_nm = sem("neg_max_ready")
        s_exp = sem("exp_ready")
        s_rs = sem("row_sum_ready")
        s_ri = sem("row_inverse_ready")
        s_th = [sem(f"p_hi_transposed{i}") for i in range(2)]
        s_tl = [sem(f"p_lo_transposed{i}") for i in range(2)]
        s_hi = sem("p_hi_ready")
        s_lo = sem("p_lo_ready")
        s_pv = sem("pv_ready")
        s_ot = sem("o_t_ready")
        s_ctj = sem("context_transposed")
        s_gj = sem("queries_projected")
        s_gv = sem("queries_copied")
        s_fin = sem("output_projected")
        s_z = sem("residual_added")
        s_st = sem("stats_ready")
        s_ag = sem("mean_var_ready")
        s_vp = sem("var_plus_eps_ready")
        s_rd = sem("rstd_ready")
        s_zn = sem("normed_ready")
        s_zg = sem("gamma_applied")
        s_y = sem("y_ready")
        s_out = [sem(f"stored{i}") for i in range(2)]
        s_idle = sem("waited_apart")

        XG = 4
        J_X = 4
        J_A = J_X + 1
        J_B = J_A + NG
        J_C = J_B + 2
        J_G = J_C + NT
        J_V = J_G + NG
        J_XR = J_V + 2
        J_M = J_XR + B // XG - 1
        J_R = J_M + NG
        N_PRO = J_R + 1
        N_SMALL = 6
        BY_VECTOR = [k for k in range(N_PRO) if J_C <= k < J_V or k % 2 == 0]
        BY_SCALAR = [k for k in range(N_PRO) if k not in BY_VECTOR]

        def job_bank(k):
            return ps[:, k % 4 if k < J_V else 4 + (k - J_V) % 4, :]

        SCALE = float(HEAD_DIM) ** -0.5

        def every_other(g):
            first = g // 2 * 2 * HG + g % 2
            return slice(first, first + 2 * HG - 1, 2)

        def context_landed(b, par):
            return 32 * (b // UNROLL + 1) if isinstance(b, int) else 16 * (b - par) + 32

        def exists(k, slot, first, last):
            return (slot >= k or not first) and (slot - k < SLOTS or not last)

        def places(last):
            return range(SLOTS + (LAG if last else 0))

        def halves(t, slot):
            return 16 * (t * SLOTS // 2 + slot // 2 + 1) if isinstance(t, int) else 8 * SLOTS * t + 16 * (slot // 2 + 1)

        def batch_of(t, slot):
            return t * UNROLL + slot // NBLK

        def buffer_of(slot):
            j = slot % NBLK
            return j if j < 4 else (j - 4) % 3

        def previous(t, slot):
            return (t, slot) if slot >= 0 else (t - 1, slot + SLOTS)

        def emptied(eng, k):
            if k in BY_VECTOR:
                eng.wait_ge(s_evd, BY_VECTOR.index(k) + 1)
            else:
                eng.wait_ge(s_eva, BY_SCALAR.index(k) + 1)

        def wait_apart(eng, counter, value):
            eng.wait_ge(counter, value)
            if not isinstance(value, int):
                eng.sem_inc(s_idle, 1)

        block = es.enter_context(nc.Block())

        def turns(eng, step):
            step(0, True, False)
            with eng.Fori(1, TURNS - 1) as t:
                step(t, False, False)
            step(TURNS - 1, False, True)

        @block.sync
        def _(sp):
            def load_context(b, par):
                whole = ctx_in[bass.ds(b, 1), 0:(KT - 1) * P, :].rearrange("o (t p) d -> p (o t) d", p=P)
                tail = ctx_in[bass.ds(b, 1), (KT - 1) * P:KL, :].rearrange("o p d -> p o d")
                sp.dma_start(c_raw[:, par, 0:KT - 1, :], whole).then_inc(s_c[par], 16)
                sp.dma_start(c_raw[0:KTAIL, par, KT - 1:KT, :], tail).then_inc(s_c[par], 16)

            sp.sem_inc(s_out[1], 16)
            sp.dma_start(w_raw[0][:, :], Wq).then_inc(s_w[0], 16)
            sp.dma_start(x_sb[:, 0:XG, :], x[0:XG, :, :].rearrange("b q d -> q b d")).then_inc(s_x[0], 16)
            sp.wait_ge(s_zero, 1)
            load_context(0, 0)
            sp.dma_start(w_raw[2][:, :], Wv).then_inc(s_w[2], 16)
            sp.dma_start(wo_sb[:, :, :], Wo.rearrange("(c p) o -> p c o", p=P)).then_inc(s_small, 16)
            sp.dma_start(x_sb[:, XG:B, :], x[XG:B, :, :].rearrange("b q d -> q b d")).then_inc(s_x[1], 16)
            load_context(1, 1)

            def transpose_parts(n, slot, parts, out, s_ready, s_done, has_older):
                par = slot % 2
                wait_apart(sp, s_ready, n + 1)
                if has_older:
                    wait_apart(sp, s_pv, n - 1)
                sp.dma_start_transpose(out[:, par, :, :], parts[:, par, :]).then_inc(s_done[par], 16)

            def step(t, first, last):
                b_next = [t * UNROLL + u + UNROLL if first or last else sp.snap(t * UNROLL + u + UNROLL)
                          for u in range(UNROLL)]
                b_done = [t * UNROLL + u - 1 if first or last else sp.snap(t * UNROLL + u - 1)
                          for u in range(UNROLL)]
                for slot in places(last):
                    n, j, u = t * SLOTS + slot, slot % NBLK, slot // NBLK
                    b = t * UNROLL + u
                    if exists(2, slot, first, last):
                        transpose_parts(n - 2, (slot - 2) % SLOTS, p_lo, pt_lo, s_lo, s_tl, not first or slot > 3)
                    if exists(1, slot, first, last):
                        transpose_parts(n - 1, (slot - 1) % SLOTS, p_hi, pt_hi, s_hi, s_th, not first or slot > 2)
                    if j == LOAD_AT and slot < SLOTS and not last:
                        wait_apart(sp, s_chl, b + 1)
                        if first and u == 0:
                            sp.wait_ge(s_fill, J_C + NT)
                        else:
                            wait_apart(sp, s_ctj, NT * b)
                        load_context(b_next[u], u)
                    if j == STORE_AT and slot < SLOTS and not (first and u == 0):
                        wait_apart(sp, s_y, b + 1)
                        sp.dma_start(out[bass.ds(b_done[u], 1), :, :].rearrange("o q d -> q o d"),
                                     y[:, (u + 1) % 2:(u + 1) % 2 + 1, :]).then_inc(s_out[(u + 1) % 2], 16)

            turns(sp, step)
            sp.wait_ge(s_y, B + 1)
            sp.dma_start(out[B - 1, :, :], y[:, (B - 1) % 2, :]).then_inc(s_out[(B - 1) % 2], 16)
            sp.wait_ge(s_out[0], 16 * TURNS)
            sp.wait_ge(s_out[1], 16 * (TURNS + 1))

        @block.tensor
        def _(pe):
            def take(k):
                if k >= J_V + 4 or 4 <= k < J_V:
                    emptied(pe, k - 4)
                return job_bank(k)

            def half_rows(h):
                return slice(HEAD_DIM * (h % 2), HEAD_DIM * (h % 2) + HEAD_DIM)

            def transpose_context(bank, par, g):
                for c in range(TG):
                    mm = pe.transpose(bank[:, c * P:(c + 1) * P], c_raw[:, par, TG * g + c, :], ident[:, :])
                return mm

            def project_queries(bank, b, g):
                for c in range(HG):
                    mm = pe.matmul(bank[:, c * QL:(c + 1) * QL], a_sb[:, HG * g + c, :],
                                   xT[:, bass.ds(b, 1), :].rearrange("p o q -> p (o q)"), start=True, stop=True)
                return mm

            def project_out(bank, par, heads):
                for h in heads:
                    mm = pe.matmul(bank[0:QL, 0:P], o_t[:, par, h * QL:(h + 1) * QL], m_sb[:, h, :],
                                   start=(h == 0), stop=(h == H - 1), skip_group_check=True)
                return mm

            def transpose_weights(i, k):
                pe.wait_ge(s_w[i], 16)
                for half in range(2):
                    bank = take(k + half)
                    for c in range(4):
                        col = (4 * half + c) * P
                        mm = pe.transpose(bank[:, c * P:(c + 1) * P], w_raw[i][:, col:col + P], ident[:, :])
                    mm.then_inc(s_fill, 1)

            def transpose_x(g, k):
                bank = take(k)
                for c in range(XG):
                    mm = pe.transpose(bank[:, c * QL:(c + 1) * QL], x_sb[:, XG * g + c, :], ident[0:QL, 0:QL])
                mm.then_inc(s_fill, 1)

            def head_products(lhs, rhs, k):
                for g in range(NG):
                    bank = take(k + g)
                    for c, h in enumerate(range(H)[every_other(g)]):
                        mm = pe.matmul(bank[:, c * P:(c + 1) * P], lhs[half_rows(h), h // 2, :],
                                       rhs[half_rows(h), h // 2, :], start=True, stop=True)
                    mm.then_inc(s_fill, 1)

            pe.wait_ge(s_ident, 1)
            transpose_weights(0, 0)
            transpose_weights(1, 2)
            pe.wait_ge(s_x[0], 16)
            transpose_x(0, J_X)
            for k in range(J_X):
                emptied(pe, k)
            head_products(w_t[0], w_t[1], J_A)
            pe.wait_ge(s_small, 16 * N_SMALL)
            for odd in range(2):
                bank = take(J_B + odd)
                for c in range(PAIRS):
                    mm = pe.matmul(bank[:, c:c + 1], w_t[1][half_rows(odd), c, :], bq_sb[half_rows(odd), c:c + 1],
                                   start=True, stop=True)
                mm.then_inc(s_fill, 1)
            pe.wait_ge(s_c[0], 32)
            for g in range(NT):
                transpose_context(take(J_C + g), 0, g).then_inc(s_fill, 1)
            for k in range(J_A, J_B):
                emptied(pe, k)
            emptied(pe, J_X)
            for g in range(NG):
                project_queries(take(J_G + g), 0, g).then_inc(s_fill, 1)

            def late_jobs():
                transpose_weights(2, J_V)
                pe.wait_ge(s_x[1], 16)
                for g in range(1, B // XG):
                    transpose_x(g, J_XR + g - 1)
                for k in range(J_V, J_XR):
                    emptied(pe, k)
                head_products(w_t[2], wo_sb, J_M)
                bank = take(J_R)
                pe.wait_ge(s_const, 1)
                pe.wait_ge(s_bvw, 1)
                for c in range(PAIRS):
                    pe.matmul(bank[:, 0:P], bv_wide[:, c, :], wo_sb[:, c, :], start=(c == 0), stop=False)
                pe.matmul(bank[:, 0:P], ones_row[:, :], rows_sb[:, 0, :], start=False, stop=True)
                pe.matmul(bank[:, P:2 * P], ones_row[:, :], rows_sb[:, 1, :], start=True, stop=True)
                pe.matmul(bank[:, 2 * P:3 * P], ones_row[:, :], rows_sb[:, 2, :], start=True,
                          stop=True).then_inc(s_fill, 1)

            def scores(n, slot, has_older):
                par, row, bank = slot // NBLK, ROW0[slot % NBLK], 3 * (slot % 2)
                gh, gl = g_hi[:, par, row:row + P], g_lo[:, par, row:row + P]
                if has_older:
                    pe.wait_ge(s_exp, 2 * n - 2)
                for k in range(3):
                    a, e = KEYCUT[k], KEYCUT[k] + KEYW
                    o = ps[:, bank + k, 0:KEYW]
                    pe.matmul(o, gh, ct_hi[:, par, a:e], start=True, stop=False)
                    pe.matmul(o, gh, ct_lo[:, par, a:e], start=False, stop=False)
                    mm = pe.matmul(o, gl, ct_hi[:, par, a:e], start=False, stop=True)
                mm.then_inc(s_sc, 1)

            def weigh(n, t, slot, is_first):
                par, par_c = slot % 2, slot // NBLK
                new = NEW_ROWS[slot % NBLK]
                out_t = ps[:, O_BANK, 0:new]
                if not is_first:
                    pe.wait_ge(s_ot, n)
                if slot % NBLK == 0:
                    pe.wait_ge(s_chl, batch_of(t, slot) + 1)
                pe.wait_ge(s_th[par], halves(t, slot))
                for i in range(KT):
                    for part in range(2):
                        pe.matmul(out_t, c_hl[:, par_c, i, part * D:(part + 1) * D], pt_hi[:, par, i, P - new:P],
                                  start=(i == 0 and part == 0), stop=False)
                pe.wait_ge(s_tl[par], halves(t, slot))
                for i in range(KT):
                    mm = pe.matmul(out_t, c_hl[:, par_c, i, 0:D], pt_lo[:, par, i, P - new:P], start=False,
                                   stop=(i == KT - 1))
                mm.then_inc(s_pv, 1)

            def step(t, first, last):
                for slot in places(last):
                    n, j, u = t * SLOTS + slot, slot % NBLK, slot // NBLK
                    b = t * UNROLL + u
                    if exists(0, slot, first, last):
                        if j == 0 and not (first and u == 0):
                            pe.wait_ge(s_cts, NT * b)
                            pe.wait_ge(s_gs, b + 1)
                        scores(n, slot, not first or slot > 1)
                    if first and slot == 0:
                        late_jobs()
                        for k in range(N_PRO - 4, N_PRO):
                            emptied(pe, k)
                    if exists(LAG, slot, first, last):
                        weigh(n - LAG, *previous(t, slot - LAG), first and slot == LAG)
                    if slot >= SLOTS:
                        continue
                    bank = ps[:, JOB_BANK, :]
                    ahead, behind = not (last and u == UNROLL - 1), not (first and u == 0)
                    if CT_AT <= j < CT_AT + NT and ahead:
                        if j == CT_AT:
                            pe.wait_ge(s_c[(u + 1) % 2], 32 * (t + 1 + u))
                        else:
                            pe.wait_ge(s_cts, NT * b + j - CT_AT)
                        transpose_context(bank, (u + 1) % 2, j - CT_AT).then_inc(s_ctj, 1)
                    elif FIN_AT <= j < G_AT and behind:
                        if j == FIN_AT:
                            if ahead:
                                pe.wait_ge(s_cts, NT * (b + 1))
                            pe.wait_ge(s_ot, NBLK * b)
                        mm = project_out(bank, (u + 1) % 2, range(HG * (j - FIN_AT), HG * (j - FIN_AT + 1)))
                        if j == G_AT - 1:
                            mm.then_inc(s_fin, 1)
                    elif G_AT <= j < G_AT + NG and ahead:
                        if j > G_AT:
                            pe.wait_ge(s_gv, NG * b + j - G_AT)
                        elif behind:
                            pe.wait_ge(s_z, b)
                        else:
                            pe.wait_ge(s_cts, NT * (b + 1))
                        project_queries(bank, b + 1, j - G_AT).then_inc(s_gj, 1)

            for k in range(J_V - 4, J_V):
                emptied(pe, k)
            pe.wait_ge(s_evd, BY_VECTOR.index(J_C + NT - 1) + 1)
            pe.wait_ge(s_gs, 1)
            turns(pe, step)
            pe.wait_ge(s_ot, NBLK * B)
            project_out(ps[:, JOB_BANK, :], (B - 1) % 2, range(H)).then_inc(s_fin, 1)

        def empty_prologue(eng, jobs, s_done, copy, scaled):
            for k in jobs:
                eng.wait_ge(s_fill, k + 1)
                bank = job_bank(k)
                if k < J_X:
                    last = copy(w_t[k // 2][:, 4 * (k % 2):4 * (k % 2) + 4, :], split(bank, 4, P))
                elif k == J_X:
                    last = copy(xT[:, 0:XG, :], split(bank, XG, QL))
                elif k < J_B:
                    last = scaled(a_sb[:, every_other(k - J_A), :], split(bank, HG, P), SCALE)
                elif k < J_C:
                    last = scaled(gb_sb[:, k - J_B:H:2], bank[:, 0:PAIRS], SCALE)
                elif k < J_XR:
                    last = copy(w_t[2][:, 4 * (k - J_V):4 * (k - J_V) + 4, :], split(bank, 4, P))
                elif k < J_M:
                    g = k - J_XR + 1
                    last = copy(xT[:, XG * g:XG * g + XG, :], split(bank, XG, QL))
                elif k < J_R:
                    last = scaled(m_sb[:, every_other(k - J_M), :], split(bank, HG, P), 1.0 / P_RANGE)
                else:
                    last = copy(rows_b[:, :, :], split(bank, 3, P))
                last.then_inc(s_done, 1)

        def early(jobs):
            return [k for k in jobs if k < J_C]

        def late(jobs):
            return [k for k in jobs if k >= J_V]

        def split(bank, n, w):
            return bank[:, 0:n * w].rearrange("p (n w) -> p n w", w=w)

        @block.vector
        def _(dve):
            def add_bias(g, bank):
                heads = slice(HG * g, HG * g + HG)
                return dve.tensor_tensor(g_raw[:, heads, :], split(bank, HG, QL),
                                         gb_sb[:, heads].unsqueeze(2).to_broadcast([P, HG, QL]), ALU.add)

            def context_t_lo(par, g, bank):
                a, e = TG * P * g, min(TG * P * (g + 1), KL)
                return dve.tensor_tensor(ct_lo[:, par, a:e], bank[:, 0:e - a], ct_hi[:, par, a:e].bitcast(F32),
                                         ALU.subtract)

            dve.memset(mhalf[:, :], -0.5)
            for part in (p_hi, p_lo):
                dve.memset(part[:, :, KL:KT * P], 0.0)
            dve.memset(ones_row[:, :], 1.0).then_inc(s_const, 1)
            scaled = lambda o, i, by: dve.tensor_scalar(o, i, by, None, ALU.mult)
            empty_prologue(dve, early(BY_VECTOR), s_evd, dve.tensor_copy, scaled)
            for g in range(NT):
                dve.wait_ge(s_cth, g + 1)
                context_t_lo(0, g, job_bank(J_C + g)).then_inc(s_evd, 1)
            for k in (J_B, J_B + 1):
                emptied(dve, k)
            for g in range(NG):
                dve.wait_ge(s_fill, J_G + g + 1)
                add_bias(g, job_bank(J_G + g)).then_inc(s_evd, 1)
            for g in range(NG):
                cols = slice(HG * QL * g, HG * QL * (g + 1))
                dve.wait_ge(s_part, g + 1)
                done = dve.tensor_tensor(g_lo[:, 0, cols], g_raw[:, HG * g:HG * g + HG, :].rearrange("p h q -> p (h q)"),
                                         g_hi[:, 0, cols].bitcast(F32), ALU.subtract)
            done.then_inc(s_gs, 1)

            def row_max(n, slot):
                bank = 3 * (slot % 2)
                dve.wait_ge(s_sc, n + 1)
                dve.tensor_reduce(nmax[:, slot:slot + 1], ps[:, bank:bank + 3, 0:KEYW], AX.XY, ALU.max,
                                  negate=True).then_inc(s_nm, 1)

            def lo_part(n, t, slot, has_older):
                par = slot % 2
                dve.wait_ge(s_hi, n + 1)
                if has_older:
                    dve.wait_ge(s_tl[par], halves(t, slot) - 16)
                dve.scalar_tensor_tensor(out=p_lo[:, par, 0:KL], in0=p32[:, buffer_of(slot), :], scalar=rinv[:, slot:slot + 1],
                                         in1=p_hi[:, par, 0:KL], op0=ALU.mult, op1=ALU.subtract).then_inc(s_lo, 1)

            def row_inverse(n, slot):
                dve.wait_ge(s_exp, 2 * n + 2)
                dve.tensor_scalar(rsum[:, slot:slot + 1], psums[:, slot, 0:1], psums[:, slot, 1:2], 1.0 / P_RANGE,
                                  ALU.add, ALU.mult).then_inc(s_rs, 1)
                dve.wait_ge(s_rs, n + 1)
                dve.reciprocal(rinv[:, slot:slot + 1], rsum[:, slot:slot + 1]).then_inc(s_ri, 1)

            def context_max(b, par, g):
                if g == 0:
                    dve.wait_ge(s_c[par], context_landed(b, par))
                dve.tensor_reduce(c_max[:, g:g + 1], c_raw[:, par, TG * g:TG * g + TG, :].rearrange("p t d -> p (t d)"),
                                  AX.X, ALU.max, apply_absolute_value=True).then_inc(s_am, 1)
                if g == NT - 1:
                    dve.wait_ge(s_am, NT * b + NT)
                    dve.tensor_reduce(c_max[:, NT:NT + 1], c_max[:, 0:NT], AX.X, ALU.max).then_inc(s_cm, 1)

            def context_scale(b, par):
                dve.wait_ge(s_ca, b + 1)
                if not isinstance(b, int) or b > 1:
                    dve.wait_ge(s_ot, NBLK * (b - 1))
                dve.tensor_scalar(unscale[:, par:par + 1], c_top[:, :], C_LEAST, 1.0 / C_RANGE, ALU.max,
                                  ALU.mult).then_inc(s_us, 1)
                dve.wait_ge(s_us, b + 1)
                dve.reciprocal(alpha[:, par:par + 1], unscale[:, par:par + 1]).then_inc(s_al, 1)

            def take_context(b, par, g):
                dve.wait_ge(s_cth, NT * b + g + 1)
                context_t_lo(par, g, ps[:, JOB_BANK, :]).then_inc(s_cts, 1)

            def take_queries(b, g):
                dve.wait_ge(s_gj, NG * (b - 1) + g + 1)
                if g == 0:
                    dve.wait_ge(s_gs, b)
                add_bias(g, ps[:, JOB_BANK, :]).then_inc(s_gv, 1)

            def take_rows(b, par, has_older):
                dve.wait_ge(s_fin, b + 1)
                if has_older:
                    dve.wait_ge(s_y, b)
                dve.tensor_tensor(z[:, par:par + 1, :], ps[0:QL, JOB_BANK, 0:D].unsqueeze(1), x_sb[:, bass.ds(b, 1), :],
                                  ALU.add).then_inc(s_z, 1)
                dve.wait_ge(s_z, b + 1)
                dve.bn_stats(stats[:, par, :], z[:, par, :]).then_inc(s_st, 1)
                wait_apart(dve, s_st, b + 1)
                dve.bn_aggr(mv[:, par, :], stats[:, par, :]).then_inc(s_ag, 1)

            def norm_rows(b, par):
                dve.wait_ge(s_rd, b + 1)
                dve.tensor_scalar(zn[:, par, :], z[:, par, :], mv[:, par, 0:1], rstd[:, par:par + 1], ALU.subtract,
                                  ALU.mult).then_inc(s_zn, 1)

            def step(t, first, last):
                for slot in places(last):
                    n, j, u = t * SLOTS + slot, slot % NBLK, slot // NBLK
                    b = t * UNROLL + u
                    ahead = slot < SLOTS and not (last and u == UNROLL - 1)
                    if exists(0, slot, first, last):
                        row_max(n, slot)
                    if first and slot == 0:
                        before_loop()
                    if CT_AT < j <= CT_AT + NT and ahead:
                        take_context(b + 1, (u + 1) % 2, j - CT_AT - 1)
                    if j == ROWS_AT and slot < SLOTS and not (first and u == 0):
                        take_rows(b - 1, (u + 1) % 2, not first)
                    if exists(1, slot, first, last):
                        row_inverse(n - 1, (slot - 1) % SLOTS)
                    if exists(2, slot, first, last):
                        lo_part(n - 2, *previous(t, slot - 2), not first or slot > 3)
                    if slot >= SLOTS:
                        continue
                    if CMAX_AT <= j < CMAX_AT + NT and ahead:
                        context_max(b + 1, (u + 1) % 2, j - CMAX_AT)
                    elif j == SCALE_AT and ahead:
                        context_scale(b + 1, (u + 1) % 2)
                    if G_AT <= j < G_AT + NG and ahead:
                        take_queries(b + 1, j - G_AT)
                    if j == NORM_AT and not (first and u == 0):
                        norm_rows(b - 1, (u + 1) % 2)

            for g in range(NT):
                context_max(0, 0, g)

            def before_loop():
                context_scale(0, 0)
                dve.wait_ge(s_small, 16 * N_SMALL)
                dve.tensor_copy(bv_wide[:, :, :],
                                bv_sb[:, :].unsqueeze(2).to_broadcast([P, PAIRS, P])).then_inc(s_bvw, 1)
                empty_prologue(dve, late(BY_VECTOR), s_evd, dve.tensor_copy, scaled)

            turns(dve, step)
            take_rows(B - 1, (B - 1) % 2, True)
            norm_rows(B - 1, (B - 1) % 2)

        @block.scalar
        def _(act):
            act.dma_start(w_raw[1][:, :], Wk).then_inc(s_w[1], 16)
            act.dma_start(bq_sb[:, :], bq.rearrange("(c p) -> p c", p=P), allow_slow_non_contiguous=True).then_inc(s_small, 16)
            act.dma_start(bv_sb[:, :], bv.rearrange("(c p) -> p c", p=P), allow_slow_non_contiguous=True).then_inc(s_small, 16)
            for i, r in enumerate((bo, gamma, beta)):
                act.dma_start(rows_sb[:, i, :], r.rearrange("(o d) -> o d", o=1)).then_inc(s_small, 16)

            def context_t_hi(par, g, bank):
                a, e = TG * P * g, min(TG * P * (g + 1), KL)
                act.copy(ct_hi[:, par, a:e], bank[:, 0:e - a]).then_inc(s_cth, 1)

            scaled = lambda o, i, by: act.mul(o, i, by)
            empty_prologue(act, early(BY_SCALAR), s_eva, act.copy, scaled)
            for g in range(NT):
                act.wait_ge(s_fill, J_C + g + 1)
                context_t_hi(0, g, job_bank(J_C + g))
            for g in range(NG):
                emptied(act, J_G + g)
                cols = slice(HG * QL * g, HG * QL * (g + 1))
                act.copy(g_hi[:, 0, cols], g_raw[:, HG * g:HG * g + HG, :].rearrange("p h q -> p (h q)")).then_inc(s_part, 1)

            def exponentials(n, slot, has_older):
                buf, bank = buffer_of(slot), 3 * (slot % 2)
                act.wait_ge(s_nm, n + 1)
                if has_older:
                    act.wait_ge(s_lo, n - 2)
                act.activation(p32[:, buf, 0:2 * KEYW].rearrange("p (k w) -> p k w", w=KEYW), ps[:, bank:bank + 2, 0:KEYW],
                               ACT.Exp, bias=nmax[:, slot:slot + 1], accum_out=psums[:, slot, 0:1]).then_inc(s_exp, 1)
                act.activation(p32[:, buf, 2 * KEYW:KL], ps[:, bank + 2, TWICE:KEYW], ACT.Exp,
                               bias=nmax[:, slot:slot + 1], accum_out=psums[:, slot, 1:2]).then_inc(s_exp, 1)

            def hi_part(n, t, slot, has_older):
                par = slot % 2
                act.wait_ge(s_ri, n + 1)
                if has_older:
                    act.wait_ge(s_th[par], halves(t, slot) - 16)
                act.activation(p_hi[:, par, 0:KL], p32[:, buffer_of(slot), :], ACT.Copy, scale=rinv[:, slot:slot + 1]).then_inc(s_hi, 1)

            def context_hi(b, par, g):
                if g == 0:
                    act.wait_ge(s_al, b + 1)
                    if not isinstance(b, int) or b > 1:
                        act.wait_ge(s_pv, NBLK * (b - 1))
                tiles = slice(TG * g, TG * g + TG)
                act.activation(c_hl[:, par, tiles, 0:D], c_raw[:, par, tiles, :], ACT.Copy,
                               scale=alpha[:, par:par + 1]).then_inc(s_chi, 1)

            def take_result(n, slot, b, has_older):
                act.wait_ge(s_pv, n + 1)
                j, par = slot % NBLK, slot // NBLK
                if j == 0 and has_older:
                    act.wait_ge(s_fin, b - 1)
                end, new = ROW0[j] + P, NEW_ROWS[j]
                act.activation(o_t[:, par, end - new:end], ps[:, O_BANK, 0:new], ACT.Copy,
                               scale=unscale[:, par:par + 1]).then_inc(s_ot, 1)

            def step(t, first, last):
                for slot in places(last):
                    n, j, u = t * SLOTS + slot, slot % NBLK, slot // NBLK
                    b, done = t * UNROLL + u, slot - LAG
                    ahead = slot < SLOTS and not (last and u == UNROLL - 1)
                    if exists(LAG, slot, first, last):
                        take_result(n - LAG, done % SLOTS, batch_of(t, done), not first)
                    if exists(0, slot, first, last):
                        exponentials(n, slot, not first or slot > 2)
                    if first and slot == 0:
                        for g in range(NT):
                            context_hi(0, 0, g)
                        empty_prologue(act, late(BY_SCALAR), s_eva, act.copy, scaled)
                    if CT_AT <= j < CT_AT + NT and ahead:
                        act.wait_ge(s_ctj, NT * b + j - CT_AT + 1)
                        context_t_hi((u + 1) % 2, j - CT_AT, ps[:, JOB_BANK, :])
                    if exists(1, slot, first, last):
                        hi_part(n - 1, *previous(t, slot - 1), not first or slot > 2)
                    if CHI_AT <= j < CHI_AT + NT and ahead:
                        context_hi(b + 1, (u + 1) % 2, j - CHI_AT)

            turns(act, step)

        @block.gpsimd
        def _(pool):
            pool.sem_inc(s_y, 1)
            pool.memset(ident[:, :], 0.0).then_inc(s_id0, 1)
            pool.wait_ge(s_id0, 1)
            pool.affine_select(out=ident[:, :], in_=ident[:, :], compare_op=ALU.not_equal, fill=1.0, base=0,
                               pattern=[[-1, P]], channel_multiplier=1).then_inc(s_ident, 1)
            pool.memset(c_raw[:, :, KT - 1, :], 0.0).then_inc(s_zero, 1)

            def split_parts(hi, lo, raw, count, s_done):
                pool.tensor_copy(hi, raw).then_inc(s_part, 1)
                wait_apart(pool, s_part, count)
                done = pool.tensor_tensor(lo, raw, hi.bitcast(F32), ALU.subtract)
                if s_done is not None:
                    done.then_inc(s_done, 1)

            def context_top(b):
                wait_apart(pool, s_cm, b + 1)
                pool.partition_all_reduce(c_top[:, :], c_max[:, NT:NT + 1], P, RMAX).then_inc(s_ca, 1)

            def context_lo(b, par):
                wait_apart(pool, s_chi, NT * b + NT)
                flat = "p t d -> p (t d)"
                pool.tensor_scalar(c_scaled[:, :], c_raw[:, par, :, :].rearrange(flat), alpha[:, par:par + 1], 1.0,
                                   ALU.mult, ALU.mult).then_inc(s_cs, 1)
                wait_apart(pool, s_cs, b + 1)
                pool.tensor_tensor(c_hl[:, par, :, D:2 * D], c_scaled[:, :].rearrange("p (t d) -> p t d", d=D),
                                   c_hl[:, par, :, 0:D], ALU.subtract).then_inc(s_chl, 1)

            def split_queries(b, par, g):
                cols = slice(HG * QL * g, HG * QL * (g + 1))
                split_parts(g_hi[:, par, cols], g_lo[:, par, cols],
                            g_raw[:, HG * g:HG * g + HG, :].rearrange("p h q -> p (h q)"), NG * b + g + 1,
                            s_gs if g == NG - 1 else None)

            def inverse_deviation(b, par):
                wait_apart(pool, s_ag, b + 1)
                pool.tensor_scalar(vpe[:, par:par + 1], mv[:, par, 1:2], EPS, None, ALU.add).then_inc(s_vp, 1)
                wait_apart(pool, s_vp, b + 1)
                pool.tensor_tensor(rstd[:, par:par + 1], vpe[:, par:par + 1], mhalf[:, :], ALU.pow).then_inc(s_rd, 1)

            def scale_rows(b, par, counted):
                wait_apart(pool, s_zn, b + 1)
                pool.tensor_tensor(zg[:, par, :], zn[:, par, :], rows_b[0:QL, 1, :], ALU.mult).then_inc(s_zg, 1)
                wait_apart(pool, s_zg, b + 1)
                if not isinstance(counted, int) or counted > 0:
                    wait_apart(pool, s_out[par], 16 * counted)
                pool.tensor_tensor(y[:, par, :], zg[:, par, :], rows_b[0:QL, 2, :], ALU.add).then_inc(s_y, 1)

            context_top(0)
            context_lo(0, 0)
            emptied(pool, J_R)
            emptied(pool, J_M - 1)
            emptied(pool, J_M - 2)
            pool.tensor_tensor(x_sb[:, :, :], x_sb[:, :, :], rows_b[0:QL, 0:1, :].to_broadcast([QL, B, D]),
                               ALU.add).then_inc(s_xres, 1)
            def step(t, first, last):
                for u in range(UNROLL):
                    b, other = t * UNROLL + u, (u + 1) % 2
                    if not (last and u == UNROLL - 1):
                        context_top(b + 1)
                    if not (first and u == 0):
                        inverse_deviation(b - 1, other)
                    if not (last and u == UNROLL - 1):
                        for g in range(NG):
                            wait_apart(pool, s_gv, NG * b + g + 1)
                            split_queries(b + 1, other, g)
                    if not (first and u == 0):
                        scale_rows(b - 1, other, t)
                    if not (last and u == UNROLL - 1):
                        context_lo(b + 1, other)

            turns(pool, step)
            inverse_deviation(B - 1, (B - 1) % 2)
            scale_rows(B - 1, (B - 1) % 2, TURNS)


_INS = ['x', 'ctx_1024', 'L0_xattn_Wq', 'L0_xattn_bq', 'L0_xattn_Wk', 'L0_xattn_bk', 'L0_xattn_Wv', 'L0_xattn_bv',
        'L0_xattn_Wo', 'L0_xattn_bo', 'L0_xattn_gamma', 'L0_xattn_beta']
_OUTS = [((16, 100, 128), 'float32')]


def kernel(**inputs):
    import numpy as _np
    import concourse.bacc as _bacc
    from concourse import mybir as _mybir
    from concourse.bass_utils import run_bass_kernel_spmd as _run

    nc = _bacc.Bacc("TRN2", target_bir_lowering=False, num_devices=1)
    arrays, args = {}, []
    for name in _INS:
        a = _np.ascontiguousarray(inputs[name])
        arrays[f"in_{name}_dram"] = a
        args.append(nc.dram_tensor(f"in_{name}_dram", a.shape, _mybir.dt.from_np(a.dtype), kind="ExternalInput").ap())
    for i, (shape, dtype) in enumerate(_OUTS):
        dt = _mybir.dt.from_np(_np.dtype(dtype))
        args.append(nc.dram_tensor(f"out_{i}_dram", shape, dt, kind="ExternalOutput").ap())
    cross_attention_kernel(nc, *args)
    r = _run(nc, [arrays], core_ids=[0])
    got = tuple(r.results[0][f"out_{i}_dram"] for i in range(len(_OUTS)))
    return got[0]
```

```python
from contextlib import ExitStack

import concourse.bass as bass
from concourse import mybir

ALU = mybir.AluOpType
ACT = mybir.ActivationFunctionType
AX = mybir.AxisListType
F32 = mybir.dt.float32
F32R = mybir.dt.float32r
F16 = mybir.dt.float16

P = 128
HEAD_DIM = 64
EPS = 1e-5
RMAX = bass.bass_isa.ReduceOp.max
C_RANGE = 2.0 ** 14
P_RANGE = 2.0 ** 14
C_LEAST = 1e-30
UNROLL = 2


def cross_attention_kernel(nc, x, ctx_in, Wq, bq, Wk, bk, Wv, bv, Wo, bo, gamma, beta, out):
    B, QL, D = x.shape
    KL = ctx_in.shape[1]
    H = Wq.shape[1] // HEAD_DIM
    D_H = H * HEAD_DIM
    PAIRS = H // 2
    ROWS = H * QL
    KT = -(-KL // P)
    KTAIL = KL - (KT - 1) * P
    assert 3 * KTAIL <= P
    NBLK = -(-ROWS // P)
    ROW0 = [min(P * j, ROWS - P) for j in range(NBLK)]
    NEW_ROWS = [P] * (NBLK - 1) + [ROWS - P * (NBLK - 1)]
    KEYW = 482
    KEYCUT = [0, KEYW, KL - KEYW]
    TWICE = 3 * KEYW - KL
    LAG = 4
    LOADS = 6
    TG = 4
    NT = KT // TG
    HG = 4
    NG = H // HG
    SLOTS = UNROLL * NBLK
    TURNS = B // UNROLL
    CT_AT = 0
    FIN_AT = LAG
    ROWS_AT = FIN_AT + NG
    G_AT = ROWS_AT + 1
    NORM_AT = ROWS_AT + 2
    CMAX_AT = FIN_AT
    SCALE_AT = CMAX_AT + NT + 1
    CHI_AT = SCALE_AT + 1
    LOAD_AT = FIN_AT
    STORE_AT = NBLK - 1
    with ExitStack() as es:
        def sb(name, shape, dt=F32):
            return es.enter_context(nc.sbuf_tensor(name, shape, dt))

        def sem(name):
            return es.enter_context(nc.semaphore(name))

        ident = sb("ident", [P, P])
        early_sb = sb("early_sb", [P, 4, PAIRS, P])
        w_t = [early_sb[:, i] for i in range(3)]
        bv_wide = early_sb[:, 3]
        a16 = early_sb[:, 0:2].rearrange("p i c e -> p (i c e)").bitcast(F16).rearrange(
            "p (h i d) -> p h i d", i=2, d=P)
        x16 = early_sb[:, 2:4].rearrange("p i c e -> p (i c e)").bitcast(F16)[:, 0:2 * B * QL].rearrange(
            "p (b i q) -> p b i q", i=2, q=QL)
        wo_sb = sb("wo_sb", [P, PAIRS, P])
        gb_raw = sb("gb_raw", [P, H])
        bv_sb = sb("bv_sb", [P, PAIRS])
        ax_parts = sb("ax_parts", [P, 2, NG])
        ax_max = sb("ax_max", [P, 2])
        ax_top = sb("ax_top", [P, 2])
        ax_un = sb("ax_un", [P, 2])
        ax_scale = sb("ax_scale", [P, 2])
        g_un = sb("g_un", [P, 1])
        rows_sb = sb("rows_sb", [1, 3, P])
        ones_row = sb("ones_row", [1, P])
        table = sb("table", [P, 1])
        x_sb = sb("x_sb", [QL, B, D])
        xT = sb("xT", [P, B, QL])
        a_sb = sb("a_sb", [P, H, P])
        m_sb = sb("m_sb", [P, H, P])
        gb_sb = sb("gb_sb", [P, H])
        rows_b = sb("rows_b", [P, 3, P])
        c_raw = sb("c_raw", [P, 2, KT, D])
        c_hl = sb("c_hl", [P, 2, KT, 2 * D], F16)
        c_tail = sb("c_tail", [P, 2, D], F16)
        c_max = sb("c_max", [P, 4])
        c_scaled = sb("c_scaled", [P, KT * D])
        c_top = sb("c_top", [P, 1])
        alpha = sb("alpha", [P, 2])
        unscale = sb("unscale", [P, 2])
        ct_hi = sb("ct_hi", [P, 2, KL], F32R)
        ct_lo = sb("ct_lo", [P, 2, KL], F32R)
        g_raw = sb("g_raw", [P, H, QL])
        g_hi = sb("g_hi", [P, 2, ROWS], F32R)
        g_lo = sb("g_lo", [P, 2, ROWS], F32R)
        p32 = sb("p32", [P, 4, KL])
        bq_wide = p32[:, 3, 0:D_H]
        wk_bq = p32[:, 2, 0:D_H]
        p_hi = sb("p_hi", [P, 2, KL], F16)
        p_lo = sb("p_lo", [P, 2, KT * P], F16)
        pt_hi = sb("pt_hi", [P, 2, KT - 1, P], F16)
        pt_lo = sb("pt_lo", [P, 2, KT, P], F16)
        nmax = sb("nmax", [P, SLOTS])
        psums = sb("psums", [P, SLOTS, 2])
        rsum = sb("rsum", [P, SLOTS])
        rinv = sb("rinv", [P, SLOTS])
        o_t = sb("o_t", [P, 2, ROWS])
        w_all = o_t[:, :, :].rearrange("p a r -> p (a r)")
        w_raw = [w_all[:, i * D_H:(i + 1) * D_H] for i in range(3)]
        z = sb("z", [QL, 2, D])
        stats = sb("stats", [QL, 2, 6])
        mv = sb("mv", [QL, 2, 2])
        vpe = sb("vpe", [QL, 2])
        rstd = sb("rstd", [QL, 2])
        mhalf = sb("mhalf", [QL, 1])
        zn = sb("zn", [QL, 2, D])
        zg = sb("zg", [QL, 2, D])
        y = sb("y", [QL, 2, D])

        ps = es.enter_context(nc.psum_tensor("ps", [P, 8, 512], F32))
        O_BANK, JOB_BANK = 6, 7

        s_w = [[sem(f"w_loaded{i}_{half}") for half in range(2)] for i in range(3)]
        s_small = sem("small_loaded")
        s_x = [sem(f"x_loaded{i}") for i in range(2)]
        s_c = [sem(f"context_loaded{i}") for i in range(2)]
        s_const = sem("constants_set")
        s_id0 = sem("identity_zeroed")
        s_ident = sem("identity_ready")
        s_zero = sem("key_padding_zeroed")
        s_bvw = sem("bv_spread")
        s_part = sem("hi_part_ready")
        s_am = sem("context_group_max")
        s_cm = sem("context_partition_max")
        s_ca = sem("context_max")
        s_us = sem("unscale_ready")
        s_al = sem("alpha_ready")
        s_chi = sem("context_hi_ready")
        s_cs = sem("context_scaled")
        s_cl = sem("context_lo_steps")
        s_axz = sem("ax_parts_zeroed")
        s_ax = sem("ax_group_max")
        s_axc = sem("ax_partition_max")
        s_axa = sem("ax_max")
        s_axu = sem("ax_unscale_ready")
        s_axs = sem("ax_scale_ready")
        s_16h = sem("ax_hi_ready")
        s_16s = sem("ax_scaled")
        s_16 = sem("ax_split")
        s_fill = sem("prologue_bank_filled")
        s_evd = sem("prologue_bank_emptied_by_vector")
        s_eva = sem("prologue_bank_emptied_by_scalar")
        s_xres = sem("residual_ready")
        s_bq = sem("bq_loaded")
        s_bvl = sem("bv_loaded")
        s_wb = sem("wk_times_bq")
        s_gb = sem("gb_ready")
        s_g0 = sem("first_queries_split")
        s_chl = sem("context_split")
        s_cth = sem("context_t_hi_ready")
        s_cts = sem("context_t_split")
        s_gs = sem("g_split")
        s_sc = sem("scores_ready")
        s_nm = sem("neg_max_ready")
        s_exp = sem("exp_ready")
        s_rs = sem("row_sum_ready")
        s_ri = sem("row_inverse_ready")
        s_th = [sem(f"p_hi_transposed{i}") for i in range(2)]
        s_tl = [sem(f"p_lo_transposed{i}") for i in range(2)]
        s_hi = sem("p_hi_ready")
        s_lo = sem("p_lo_ready")
        s_pt = sem("p_hi_tail_ready")
        s_pv = sem("pv_ready")
        s_ot = sem("o_t_ready")
        s_ctj = sem("context_transposed")
        s_gj = sem("queries_projected")
        s_gv = sem("queries_copied")
        s_fin = sem("output_projected")
        s_z = sem("residual_added")
        s_st = sem("stats_ready")
        s_ag = sem("mean_var_ready")
        s_vp = sem("var_plus_eps_ready")
        s_rd = sem("rstd_ready")
        s_zn = sem("normed_ready")
        s_zg = sem("gamma_applied")
        s_y = sem("y_ready")
        s_out = [sem(f"stored{i}") for i in range(2)]
        s_idle = sem("waited_apart")

        XG = 4
        J_X = 4
        J_A = J_X + 1
        J_C = J_A + NG
        J_G = J_C + NT
        J_V = J_G + NG
        J_X1 = J_V + 2
        J_M = J_X1 + 1
        J_R = J_M + NG
        J_X2 = J_R + 1
        N_PRO = J_X2 + B // XG - 2
        ONCE = {0: J_V, 1: J_V + 1, CT_AT + NT: J_X1, ROWS_AT: J_R, NBLK + CT_AT + NT: J_X2, NBLK + ROWS_AT: J_X2 + 1}
        ONCE.update({FIN_AT + g: J_M + g for g in range(NG)})
        N_SMALL = 4
        BY_SCALAR = [1, 3, J_A + 1, J_A + 3, J_V, J_V + 1, J_M, J_M + 1, J_R]
        BY_VECTOR = [k for k in range(N_PRO) if k not in BY_SCALAR]
        WARM_UP = 12

        def job_bank(k):
            return ps[:, k % 8 if k < J_V else O_BANK if k < J_X1 else JOB_BANK, :]

        SCALE = float(HEAD_DIM) ** -0.5

        def every_other(g):
            first = g // 2 * 2 * HG + g % 2
            return slice(first, first + 2 * HG - 1, 2)

        def context_landed(b, par):
            return 16 * LOADS * (b // UNROLL + 1) if isinstance(b, int) else 8 * LOADS * (b - par) + 16 * LOADS

        def exists(k, slot, first, last):
            return (slot >= k or not first) and (slot - k < SLOTS or not last)

        def places(last):
            return range(SLOTS + (LAG if last else 0))

        def halves(t, slot):
            return 16 * (t * SLOTS // 2 + slot // 2 + 1) if isinstance(t, int) else 8 * SLOTS * t + 16 * (slot // 2 + 1)

        def batch_of(t, slot):
            return t * UNROLL + slot // NBLK

        def buffer_of(slot):
            j = slot % NBLK
            return j if j < 4 else (j - 4) % 3

        def previous(t, slot):
            return (t, slot) if slot >= 0 else (t - 1, slot + SLOTS)

        def emptied(eng, k):
            if k in BY_VECTOR:
                eng.wait_ge(s_evd, BY_VECTOR.index(k) + 1)
            else:
                eng.wait_ge(s_eva, BY_SCALAR.index(k) + 1)

        def wait_apart(eng, counter, value):
            eng.wait_ge(counter, value)
            if not isinstance(value, int):
                eng.sem_inc(s_idle, 1)

        block = es.enter_context(nc.Block())

        def turns(eng, step):
            step(0, True, False)
            with eng.Fori(1, TURNS - 1) as t:
                step(t, False, False)
            step(TURNS - 1, False, True)

        @block.sync
        def _(sp):
            def load_context(b, par, g):
                a, e = TG * g, min(TG * g + TG, KT - 1)
                whole = ctx_in[bass.ds(b, 1), a * P:e * P, :].rearrange("o (t p) d -> p (o t) d", p=P)
                sp.dma_start(c_raw[:, par, a:e, :], whole).then_inc(s_c[par], 16)
                if g == NT - 1:
                    tail = ctx_in[bass.ds(b, 1), (KT - 1) * P:KL, :].rearrange("o p d -> p o d")
                    for i in range(3):
                        sp.dma_start(c_raw[i * KTAIL:(i + 1) * KTAIL, par, KT - 1:KT, :], tail).then_inc(s_c[par], 16)

            sp.sem_inc(s_out[1], 16)
            for half in range(2):
                cols = slice(half * D_H // 2, (half + 1) * D_H // 2)
                sp.dma_start(w_raw[0][:, cols], Wq[:, cols]).then_inc(s_w[0][half], 16)
            sp.dma_start(x_sb[:, 0:XG, :], x[0:XG, :, :].rearrange("b q d -> q b d")).then_inc(s_x[0], 16)
            sp.wait_ge(s_zero, 1)
            for g in range(NT):
                load_context(0, 0, g)
            for half in range(2):
                cols = slice(half * D_H // 2, (half + 1) * D_H // 2)
                sp.dma_start(w_raw[2][:, cols], Wv[:, cols]).then_inc(s_w[2][half], 16)
            sp.dma_start(wo_sb[:, :, :], Wo.rearrange("(c p) o -> p c o", p=P)).then_inc(s_small, 16)
            sp.dma_start(bv_sb[:, :], bv.rearrange("(c p) -> p c", p=P), allow_slow_non_contiguous=True).then_inc(s_bvl, 16)
            for i, r in enumerate((bo, gamma, beta)):
                sp.dma_start(rows_sb[:, i, :], r.rearrange("(o d) -> o d", o=1)).then_inc(s_small, 16)
            sp.dma_start(x_sb[:, XG:B, :], x[XG:B, :, :].rearrange("b q d -> q b d")).then_inc(s_x[1], 16)
            for g in range(NT):
                load_context(1, 1, g)

            def transpose_parts(n, slot, parts, out, s_ready, s_done, has_older):
                par = slot % 2
                for counter in s_ready:
                    wait_apart(sp, counter, n + 1)
                if has_older:
                    wait_apart(sp, s_pv, n - 1)
                sp.dma_start_transpose(out[:, par, :, :], parts[:, par, 0:out.shape[2] * P]).then_inc(s_done[par], 16)

            def step(t, first, last):
                b_next = [t * UNROLL + u + UNROLL if first or last else sp.snap(t * UNROLL + u + UNROLL)
                          for u in range(UNROLL)]
                b_done = [t * UNROLL + u - 1 if first or last else sp.snap(t * UNROLL + u - 1)
                          for u in range(UNROLL)]
                for slot in places(last):
                    n, j, u = t * SLOTS + slot, slot % NBLK, slot // NBLK
                    b = t * UNROLL + u
                    if exists(2, slot, first, last):
                        transpose_parts(n - 2, (slot - 2) % SLOTS, p_lo, pt_lo, (s_lo, s_pt), s_tl, not first or slot > 3)
                    if exists(1, slot, first, last):
                        transpose_parts(n - 1, (slot - 1) % SLOTS, p_hi, pt_hi, (s_hi,), s_th, not first or slot > 2)
                    if LOAD_AT <= j < LOAD_AT + NT and slot < SLOTS and not last:
                        if j == LOAD_AT:
                            wait_apart(sp, s_chl, b + 1)
                            if first and u == 0:
                                sp.wait_ge(s_fill, J_C + NT)
                            else:
                                wait_apart(sp, s_ctj, NT * b)
                        load_context(b_next[u], u, j - LOAD_AT)
                    if j == STORE_AT and slot < SLOTS and not (first and u == 0):
                        wait_apart(sp, s_y, b + 1)
                        sp.dma_start(out[bass.ds(b_done[u], 1), :, :].rearrange("o q d -> q o d"),
                                     y[:, (u + 1) % 2:(u + 1) % 2 + 1, :]).then_inc(s_out[(u + 1) % 2], 16)

            turns(sp, step)
            sp.wait_ge(s_y, B + 1)
            sp.dma_start(out[B - 1, :, :], y[:, (B - 1) % 2, :]).then_inc(s_out[(B - 1) % 2], 16)
            sp.wait_ge(s_out[0], 16 * TURNS)
            sp.wait_ge(s_out[1], 16 * (TURNS + 1))

        @block.tensor
        def _(pe):
            def take(k):
                if k == J_V:
                    emptied(pe, J_G + 2)
                elif k == J_X1:
                    pe.wait_ge(s_cts, NT)
                elif k == J_X2:
                    pe.wait_ge(s_cts, 2 * NT)
                elif k == J_X2 + 1:
                    pe.wait_ge(s_z, 1)
                elif k >= 8:
                    emptied(pe, k - 1 if k > J_V else k - 8)
                return job_bank(k)

            def half_rows(h):
                return slice(HEAD_DIM * (h % 2), HEAD_DIM * (h % 2) + HEAD_DIM)

            def transpose_context(bank, par, g):
                for c in range(TG):
                    mm = pe.transpose(bank[:, c * P:(c + 1) * P], c_raw[:, par, TG * g + c, :], ident[:, :])
                return mm

            def project_queries(bank, b, g):
                for c in range(HG):
                    mm = pe.matmul(bank[:, c * QL:(c + 1) * QL], a_sb[:, HG * g + c, :],
                                   xT[:, bass.ds(b, 1), :].rearrange("p o q -> p (o q)"), start=True, stop=True)
                return mm

            def project_queries_16(bank, b, g):
                for c in range(HG):
                    for a_part, x_part in ((0, 0), (1, 0), (0, 1)):
                        mm = pe.matmul(bank[:, c * QL:(c + 1) * QL], a16[:, HG * g + c, a_part, :],
                                       x16[:, bass.ds(b, 1), x_part, :].rearrange("p o q -> p (o q)"),
                                       start=(a_part + x_part == 0), stop=(x_part == 1))
                return mm

            def project_out(bank, par, heads):
                for h in heads:
                    mm = pe.matmul(bank[0:QL, 0:P], o_t[:, par, h * QL:(h + 1) * QL], m_sb[:, h, :],
                                   start=(h == 0), stop=(h == H - 1), skip_group_check=True)
                return mm

            def transpose_weights(i, half, k):
                bank = take(k)
                pe.wait_ge(s_w[i][half], 16)
                for c in range(4):
                    col = (4 * half + c) * P
                    mm = pe.transpose(bank[:, c * P:(c + 1) * P], w_raw[i][:, col:col + P], ident[:, :])
                mm.then_inc(s_fill, 1)

            def transpose_x(g, k):
                bank = take(k)
                for c in range(XG):
                    mm = pe.transpose(bank[:, c * QL:(c + 1) * QL], x_sb[:, XG * g + c, :], ident[0:QL, 0:QL])
                mm.then_inc(s_fill, 1)

            def head_products(lhs, rhs, g, k):
                bank = take(k)
                for c, h in enumerate(range(H)[every_other(g)]):
                    mm = pe.matmul(bank[:, c * P:(c + 1) * P], lhs[half_rows(h), h // 2, :],
                                   rhs[half_rows(h), h // 2, :], start=True, stop=True)
                mm.then_inc(s_fill, 1)

            pe.wait_ge(s_ident, 1)
            for _ in range(WARM_UP):
                pe.transpose(ps[:, JOB_BANK, 0:P], ident[:, :], ident[:, :])
            for half in range(2):
                for i in range(2):
                    transpose_weights(i, half, 2 * half + i)
            pe.wait_ge(s_x[0], 16)
            transpose_x(0, J_X)
            for k in range(J_X):
                emptied(pe, k)
            for g in range(NG):
                head_products(w_t[0], w_t[1], g, J_A + g)
            pe.wait_ge(s_c[0], 16 * LOADS)
            for g in range(NT):
                transpose_context(take(J_C + g), 0, g).then_inc(s_fill, 1)
            emptied(pe, J_X)
            for k in range(J_A, J_C):
                emptied(pe, k)
            for g in range(NG):
                project_queries(take(J_G + g), 0, g).then_inc(s_fill, 1)

            def bias_rows(k):
                bank = take(k)
                pe.wait_ge(s_small, 16 * N_SMALL)
                pe.wait_ge(s_const, 1)
                pe.wait_ge(s_bvw, 1)
                for c in range(PAIRS):
                    pe.matmul(bank[:, 0:P], bv_wide[:, c, :], wo_sb[:, c, :], start=(c == 0), stop=False)
                pe.matmul(bank[:, 0:P], ones_row[:, :], rows_sb[:, 0, :], start=False, stop=True)
                pe.matmul(bank[:, P:2 * P], ones_row[:, :], rows_sb[:, 1, :], start=True, stop=True)
                pe.matmul(bank[:, 2 * P:3 * P], ones_row[:, :], rows_sb[:, 2, :], start=True,
                          stop=True).then_inc(s_fill, 1)

            def once(k):
                if k < J_X1:
                    transpose_weights(2, k - J_V, k)
                elif k == J_R:
                    bias_rows(k)
                elif J_M <= k < J_R:
                    for v in range(J_V, J_X1):
                        emptied(pe, v)
                    head_products(w_t[2], wo_sb, k - J_M, k)
                else:
                    pe.wait_ge(s_x[1], 16)
                    transpose_x(1 if k == J_X1 else k - J_X2 + 2, k)

            def scores(n, slot, has_older):
                par, row, bank = slot // NBLK, ROW0[slot % NBLK], 3 * (slot % 2)
                gh, gl = g_hi[:, par, row:row + P], g_lo[:, par, row:row + P]
                if has_older:
                    pe.wait_ge(s_exp, 2 * n - 2)
                for k in range(3):
                    a, e = KEYCUT[k], KEYCUT[k] + KEYW
                    o = ps[:, bank + k, 0:KEYW]
                    pe.matmul(o, gh, ct_hi[:, par, a:e], start=True, stop=False)
                    pe.matmul(o, gh, ct_lo[:, par, a:e], start=False, stop=False)
                    mm = pe.matmul(o, gl, ct_hi[:, par, a:e], start=False, stop=True)
                mm.then_inc(s_sc, 1)

            def weigh(n, t, slot, is_first):
                par, par_c = slot % 2, slot // NBLK
                new = NEW_ROWS[slot % NBLK]
                out_t = ps[:, O_BANK, 0:new]
                if not is_first:
                    pe.wait_ge(s_ot, n)
                if slot % NBLK == 0:
                    pe.wait_ge(s_chl, batch_of(t, slot) + 1)
                pe.wait_ge(s_th[par], halves(t, slot))
                for i in range(KT - 1):
                    for part in range(2):
                        pe.matmul(out_t, c_hl[:, par_c, i, part * D:(part + 1) * D], pt_hi[:, par, i, P - new:P],
                                  start=(i == 0 and part == 0), stop=False)
                pe.wait_ge(s_tl[par], halves(t, slot))
                for i in range(KT):
                    c = c_hl[:, par_c, i, 0:D] if i < KT - 1 else c_tail[:, par_c, :]
                    mm = pe.matmul(out_t, c, pt_lo[:, par, i, P - new:P], start=False, stop=(i == KT - 1))
                mm.then_inc(s_pv, 1)

            u_last = UNROLL - 1

            def heads_ready(slot):
                rows = [min(P * (s - LAG - NBLK), ROWS) for s in (slot - 1, slot)]
                return range(rows[0] // QL if slot > NBLK + ROWS_AT + 1 else 0, rows[1] // QL)

            def step(t, first, last):
                for slot in places(last):
                    n, j, u = t * SLOTS + slot, slot % NBLK, slot // NBLK
                    b = t * UNROLL + u
                    if exists(0, slot, first, last):
                        if j == 0 and not (first and u == 0):
                            pe.wait_ge(s_cts, NT * b)
                        if first and slot == 1:
                            for k in (J_C + 2, J_G, J_G + 1):
                                emptied(pe, k)
                        g = (ROW0[j] + P - 1) // (HG * QL)
                        if first and slot == 0:
                            pe.wait_ge(s_g0, 1)
                        elif j == 0 or g > (ROW0[j - 1] + P - 1) // (HG * QL):
                            pe.wait_ge(s_gs, NG * b + g)
                        scores(n, slot, not first or slot > 1)
                    if first and slot == LAG:
                        emptied(pe, J_X1 - 1)
                    if exists(LAG, slot, first, last):
                        weigh(n - LAG, *previous(t, slot - LAG), first and slot == LAG)
                    if last and slot > NBLK + ROWS_AT:
                        if slot == NBLK + ROWS_AT + 1:
                            pe.wait_ge(s_z, B - 1)
                        project_out(ps[:, JOB_BANK, :], u_last, heads_ready(slot))
                    if slot >= SLOTS:
                        continue
                    if first and slot in ONCE:
                        once(ONCE[slot])
                    bank = ps[:, JOB_BANK, :]
                    ahead, behind = not (last and u == UNROLL - 1), not (first and u == 0)
                    if CT_AT <= j < CT_AT + NT and ahead:
                        if j == CT_AT:
                            if first and u == 0:
                                emptied(pe, J_G + 3)
                            if behind:
                                pe.wait_ge(s_gv, NG * b)
                            pe.wait_ge(s_c[(u + 1) % 2], 16 * LOADS * (t + 1 + u))
                        else:
                            pe.wait_ge(s_cts, NT * b + j - CT_AT)
                        transpose_context(bank, (u + 1) % 2, j - CT_AT).then_inc(s_ctj, 1)
                    elif FIN_AT <= j < ROWS_AT and behind:
                        if j == FIN_AT:
                            if first:
                                for k in range(J_M, J_X2 + 1):
                                    emptied(pe, k)
                            if ahead:
                                pe.wait_ge(s_cts, NT * (b + 1))
                            pe.wait_ge(s_ot, NBLK * b)
                        mm = project_out(bank, (u + 1) % 2, range(HG * (j - FIN_AT), HG * (j - FIN_AT + 1)))
                        if j == ROWS_AT - 1:
                            mm.then_inc(s_fin, 1)
                    elif G_AT <= j < G_AT + NG and ahead:
                        if j > G_AT:
                            pe.wait_ge(s_gv, NG * b + j - G_AT)
                        else:
                            if behind:
                                pe.wait_ge(s_z, b)
                            if first:
                                emptied(pe, ONCE[slot - 1])
                        if first:
                            project_queries(bank, b + 1, j - G_AT).then_inc(s_gj, 1)
                        else:
                            if j == G_AT:
                                pe.wait_ge(s_16, 4)
                            project_queries_16(bank, b + 1, j - G_AT).then_inc(s_gj, 1)

            pe.wait_ge(s_evd, BY_VECTOR.index(J_C + NT - 1) + 1)
            turns(pe, step)
            pe.wait_ge(s_ot, NBLK * B)
            project_out(ps[:, JOB_BANK, :], u_last, heads_ready(SLOTS + LAG)).then_inc(s_fin, 1)

        def empty_prologue(eng, jobs, s_done, copy, scaled):
            for k in jobs:
                eng.wait_ge(s_fill, k + 1)
                bank = job_bank(k)
                if k < J_X:
                    last = copy(w_t[k % 2][:, 4 * (k // 2):4 * (k // 2) + 4, :], split(bank, 4, P))
                elif k == J_X:
                    last = copy(xT[:, 0:XG, :], split(bank, XG, QL))
                elif k < J_C:
                    last = scaled(a_sb[:, every_other(k - J_A), :], split(bank, HG, P), SCALE)
                elif k < J_X1:
                    last = copy(w_t[2][:, 4 * (k - J_V):4 * (k - J_V) + 4, :], split(bank, 4, P))
                elif k == J_R:
                    last = copy(rows_b[:, :, :], split(bank, 3, P))
                elif J_M <= k < J_R:
                    last = scaled(m_sb[:, every_other(k - J_M), :], split(bank, HG, P), 1.0 / P_RANGE)
                else:
                    g = 1 if k == J_X1 else k - J_X2 + 2
                    last = copy(xT[:, XG * g:XG * g + XG, :], split(bank, XG, QL))
                last.then_inc(s_done, 1)

        def split(bank, n, w):
            return bank[:, 0:n * w].rearrange("p (n w) -> p n w", w=w)

        @block.vector
        def _(dve):
            def add_bias(g, bank):
                heads = slice(HG * g, HG * g + HG)
                return dve.tensor_tensor(g_raw[:, heads, :], split(bank, HG, QL),
                                         gb_sb[:, heads].unsqueeze(2).to_broadcast([P, HG, QL]), ALU.add)

            def context_t_lo(par, g, bank):
                a, e = TG * P * g, min(TG * P * (g + 1), KL)
                return dve.tensor_tensor(ct_lo[:, par, a:e], bank[:, 0:e - a], ct_hi[:, par, a:e].bitcast(F32),
                                         ALU.subtract)

            dve.memset(mhalf[:, :], -0.5)
            dve.memset(p_lo[:, :, KL + 2 * KTAIL:KT * P], 0.0)
            dve.memset(ax_parts[:, :, :], 0.0).then_inc(s_axz, 1)
            dve.memset(ones_row[:, :], 1.0).then_inc(s_const, 1)
            scaled = lambda o, i, by: dve.tensor_scalar(o, i, by, None, ALU.mult)
            def empty(*jobs):
                empty_prologue(dve, jobs, s_evd, dve.tensor_copy, scaled)

            def context_max(b, par, g):
                if g == 0:
                    dve.wait_ge(s_c[par], context_landed(b, par))
                dve.tensor_reduce(c_max[:, g:g + 1], c_raw[:, par, TG * g:TG * g + TG, :].rearrange("p t d -> p (t d)"),
                                  AX.X, ALU.max, apply_absolute_value=True).then_inc(s_am, 1)
                if g == NT - 1:
                    dve.wait_ge(s_am, NT * b + NT)
                    dve.tensor_reduce(c_max[:, NT:NT + 1], c_max[:, 0:NT], AX.X, ALU.max).then_inc(s_cm, 1)

            empty(0, 2)
            empty(J_X)
            empty(J_A)
            context_max(0, 0, 0)
            empty(J_A + 2)
            context_max(0, 0, 1)
            dve.wait_ge(s_wb, 1)
            dve.tensor_reduce(gb_raw[:, :], wk_bq.rearrange("p (h j) -> p h j", h=H), AX.X, ALU.add).then_inc(s_gb, 1)
            dve.wait_ge(s_gb, 1)
            dve.tensor_scalar(gb_sb[:, :], gb_raw[:, :], SCALE, None, ALU.mult).then_inc(s_gb, 1)
            for g in range(NT):
                dve.wait_ge(s_cth, g + 1)
                context_t_lo(0, g, job_bank(J_C + g)).then_inc(s_evd, 1)
            dve.wait_ge(s_gb, 2)

            def first_bias(g):
                dve.wait_ge(s_fill, J_G + g + 1)
                add_bias(g, job_bank(J_G + g)).then_inc(s_evd, 1)

            for g in range(NG):
                first_bias(g)
                if g == 1:
                    dve.wait_ge(s_part, 1)
                    dve.tensor_tensor(g_lo[:, 0, 0:HG * QL], g_raw[:, 0:HG, :].rearrange("p h q -> p (h q)"),
                                      g_hi[:, 0, 0:HG * QL].bitcast(F32), ALU.subtract).then_inc(s_g0, 1)
            context_max(0, 0, NT - 1)

            def row_max(n, slot):
                bank = 3 * (slot % 2)
                dve.wait_ge(s_sc, n + 1)
                dve.tensor_reduce(nmax[:, slot:slot + 1], ps[:, bank:bank + 3, 0:KEYW], AX.XY, ALU.max,
                                  negate=True).then_inc(s_nm, 1)

            def lo_part(n, t, slot, has_older):
                par = slot % 2
                dve.wait_ge(s_hi, n + 1)
                if has_older:
                    dve.wait_ge(s_tl[par], halves(t, slot) - 16)
                dve.scalar_tensor_tensor(out=p_lo[:, par, 0:KL], in0=p32[:, buffer_of(slot), :], scalar=rinv[:, slot:slot + 1],
                                         in1=p_hi[:, par, 0:KL], op0=ALU.mult, op1=ALU.subtract).then_inc(s_lo, 1)

            def row_inverse(n, slot):
                dve.wait_ge(s_exp, 2 * n + 2)
                dve.tensor_scalar(rsum[:, slot:slot + 1], psums[:, slot, 0:1], psums[:, slot, 1:2], 1.0 / P_RANGE,
                                  ALU.add, ALU.mult).then_inc(s_rs, 1)
                dve.wait_ge(s_rs, n + 1)
                dve.reciprocal(rinv[:, slot:slot + 1], rsum[:, slot:slot + 1]).then_inc(s_ri, 1)

            def context_scale(b, par):
                dve.wait_ge(s_ca, b + 1)
                if not isinstance(b, int) or b > 1:
                    dve.wait_ge(s_ot, NBLK * (b - 1))
                dve.tensor_scalar(unscale[:, par:par + 1], c_top[:, :], C_LEAST, 1.0 / C_RANGE, ALU.max,
                                  ALU.mult).then_inc(s_us, 1)
                dve.wait_ge(s_us, b + 1)
                dve.reciprocal(alpha[:, par:par + 1], unscale[:, par:par + 1]).then_inc(s_al, 1)

            def take_context(b, par, g):
                dve.wait_ge(s_cth, NT * b + g + 1)
                context_t_lo(par, g, ps[:, JOB_BANK, :]).then_inc(s_cts, 1)

            def take_queries(b, g, in_parts):
                dve.wait_ge(s_gj, NG * (b - 1) + g + 1)
                if g == 0:
                    dve.wait_ge(s_gs, NG * b - 1)
                if in_parts:
                    heads = slice(HG * g, HG * g + HG)
                    done = dve.scalar_tensor_tensor(
                        out=g_raw[:, heads, :], in0=split(ps[:, JOB_BANK, :], HG, QL), scalar=g_un[:, 0:1],
                        in1=gb_sb[:, heads].unsqueeze(2).to_broadcast([P, HG, QL]), op0=ALU.mult, op1=ALU.add)
                else:
                    done = add_bias(g, ps[:, JOB_BANK, :])
                done.then_inc(s_gv, 1)

            def parts_max(g):
                if g < NG:
                    data, out = a_sb[:, HG * g:HG * g + HG, :], ax_parts[:, 0, g:g + 1]
                    for k in range(J_A, J_C):
                        emptied(dve, k)
                else:
                    data, out = x_sb[:, XG * (g - NG):XG * (g - NG) + XG, :], ax_parts[0:QL, 1, g - NG:g - NG + 1]
                    dve.wait_ge(s_x[1], 16)
                    dve.wait_ge(s_axz, 1)
                dve.tensor_reduce(out, data.rearrange("p i d -> p (i d)"), AX.X, ALU.max,
                                  apply_absolute_value=True).then_inc(s_ax, 1)
                if g == 2 * NG - 1:
                    dve.wait_ge(s_ax, 2 * NG)
                    dve.tensor_reduce(ax_max[:, :], ax_parts[:, :, :], AX.X, ALU.max).then_inc(s_axc, 1)

            def parts_scale():
                dve.wait_ge(s_axa, 1)
                dve.tensor_scalar(ax_un[:, :], ax_top[:, :], C_LEAST, 1.0 / C_RANGE, ALU.max, ALU.mult).then_inc(s_axu, 1)
                dve.wait_ge(s_axu, 1)
                dve.tensor_tensor(g_un[:, :], ax_un[:, 0:1], ax_un[:, 1:2], ALU.mult).then_inc(s_axs, 1)
                dve.reciprocal(ax_scale[:, :], ax_un[:, :]).then_inc(s_axs, 1)

            def take_rows(b, par, has_older):
                dve.wait_ge(s_fin, b + 1)
                dve.wait_ge(s_xres, 2 if has_older else 1)
                if has_older:
                    dve.wait_ge(s_y, b)
                dve.tensor_tensor(z[:, par:par + 1, :], ps[0:QL, JOB_BANK, 0:D].unsqueeze(1), x_sb[:, bass.ds(b, 1), :],
                                  ALU.add).then_inc(s_z, 1)
                dve.wait_ge(s_z, b + 1)
                dve.bn_stats(stats[:, par, :], z[:, par, :]).then_inc(s_st, 1)
                wait_apart(dve, s_st, b + 1)
                dve.bn_aggr(mv[:, par, :], stats[:, par, :]).then_inc(s_ag, 1)

            def norm_rows(b, par):
                dve.wait_ge(s_rd, b + 1)
                dve.tensor_scalar(zn[:, par, :], z[:, par, :], mv[:, par, 0:1], rstd[:, par:par + 1], ALU.subtract,
                                  ALU.mult).then_inc(s_zn, 1)

            def step(t, first, last):
                for slot in places(last):
                    n, j, u = t * SLOTS + slot, slot % NBLK, slot // NBLK
                    b = t * UNROLL + u
                    ahead = slot < SLOTS and not (last and u == UNROLL - 1)
                    if CT_AT < j <= CT_AT + NT and ahead:
                        take_context(b + 1, (u + 1) % 2, j - CT_AT - 1)
                    if exists(0, slot, first, last):
                        row_max(n, slot)
                    if first and slot == 0:
                        context_scale(0, 0)
                    if j == ROWS_AT and slot < SLOTS and not (first and u == 0):
                        take_rows(b - 1, (u + 1) % 2, not first)
                    if exists(1, slot, first, last):
                        row_inverse(n - 1, (slot - 1) % SLOTS)
                    if exists(2, slot, first, last):
                        lo_part(n - 2, *previous(t, slot - 2), not first or slot > 3)
                    if first and ONCE.get(slot) in BY_VECTOR:
                        empty(ONCE[slot])
                    if first and FIN_AT < slot <= FIN_AT + 2 * NG:
                        parts_max(slot - FIN_AT - 1)
                    elif first and slot == FIN_AT + 2 * NG + 2:
                        parts_scale()
                    if slot >= SLOTS:
                        continue
                    if CMAX_AT <= j < CMAX_AT + NT and ahead:
                        context_max(b + 1, (u + 1) % 2, j - CMAX_AT)
                    elif j == SCALE_AT and ahead:
                        context_scale(b + 1, (u + 1) % 2)
                    if G_AT <= j < G_AT + NG and ahead:
                        take_queries(b + 1, j - G_AT, not first)
                    if j == NORM_AT and not (first and u == 0):
                        norm_rows(b - 1, (u + 1) % 2)


            turns(dve, step)
            take_rows(B - 1, (B - 1) % 2, True)
            norm_rows(B - 1, (B - 1) % 2)

        @block.scalar
        def _(act):
            for half in range(2):
                cols = slice(half * D_H // 2, (half + 1) * D_H // 2)
                act.dma_start(w_raw[1][:, cols], Wk[:, cols]).then_inc(s_w[1][half], 16)
            act.dma_start(bq_wide, bq.rearrange("(o d) -> o d", o=1).to_broadcast([P, D_H])).then_inc(s_bq, 16)
            act.wait_ge(s_ident, 1)
            act.activation(table[:, :], ident[:, 0:1], ACT.Exp)

            def context_t_hi(par, g, bank):
                a, e = TG * P * g, min(TG * P * (g + 1), KL)
                act.copy(ct_hi[:, par, a:e], bank[:, 0:e - a]).then_inc(s_cth, 1)

            scaled = lambda o, i, by: act.mul(o, i, by)
            empty_prologue(act, (1, 3), s_eva, act.copy, scaled)
            empty_prologue(act, (J_A + 1, J_A + 3), s_eva, act.copy, scaled)
            for g in range(NT):
                act.wait_ge(s_fill, J_C + g + 1)
                context_t_hi(0, g, job_bank(J_C + g))
            for g in range(NG):
                emptied(act, J_G + g)
                cols = slice(HG * QL * g, HG * QL * (g + 1))
                act.copy(g_hi[:, 0, cols], g_raw[:, HG * g:HG * g + HG, :].rearrange("p h q -> p (h q)")).then_inc(s_part, 1)

            def exponentials(n, slot, has_older):
                buf, bank = buffer_of(slot), 3 * (slot % 2)
                act.wait_ge(s_nm, n + 1)
                if has_older:
                    act.wait_ge(s_lo, n - 2)
                act.activation(p32[:, buf, 0:2 * KEYW].rearrange("p (k w) -> p k w", w=KEYW), ps[:, bank:bank + 2, 0:KEYW],
                               ACT.Exp, bias=nmax[:, slot:slot + 1], accum_out=psums[:, slot, 0:1]).then_inc(s_exp, 1)
                act.activation(p32[:, buf, 2 * KEYW:KL], ps[:, bank + 2, TWICE:KEYW], ACT.Exp,
                               bias=nmax[:, slot:slot + 1], accum_out=psums[:, slot, 1:2]).then_inc(s_exp, 1)

            def hi_part(n, t, slot, has_older):
                par = slot % 2
                act.wait_ge(s_ri, n + 1)
                if has_older:
                    act.wait_ge(s_th[par], halves(t, slot) - 16)
                act.activation(p_hi[:, par, 0:KL], p32[:, buffer_of(slot), :], ACT.Copy, scale=rinv[:, slot:slot + 1]).then_inc(s_hi, 1)
                if has_older:
                    act.wait_ge(s_tl[par], halves(t, slot) - 16)
                tail = p32[:, buffer_of(slot), (KT - 1) * P:KL].unsqueeze(1).to_broadcast([P, 2, KTAIL])
                act.activation(p_lo[:, par, KL:KL + 2 * KTAIL].rearrange("p (i k) -> p i k", i=2), tail, ACT.Copy,
                               scale=rinv[:, slot:slot + 1]).then_inc(s_pt, 1)

            def context_hi(b, par, g):
                if g == 0:
                    act.wait_ge(s_al, b + 1)
                    if not isinstance(b, int) or b > 1:
                        act.wait_ge(s_pv, NBLK * (b - 1))
                tiles = slice(TG * g, TG * g + TG)
                act.activation(c_hl[:, par, tiles, 0:D], c_raw[:, par, tiles, :], ACT.Copy,
                               scale=alpha[:, par:par + 1]).then_inc(s_chi, 1)

            def take_result(n, slot, b, has_older):
                act.wait_ge(s_pv, n + 1)
                j, par = slot % NBLK, slot // NBLK
                if j == 0 and has_older:
                    act.wait_ge(s_fin, b - 1)
                end, new = ROW0[j] + P, NEW_ROWS[j]
                act.activation(o_t[:, par, end - new:end], ps[:, O_BANK, 0:new], ACT.Copy,
                               scale=unscale[:, par:par + 1]).then_inc(s_ot, 1)

            def step(t, first, last):
                for slot in places(last):
                    n, j, u = t * SLOTS + slot, slot % NBLK, slot // NBLK
                    b, done = t * UNROLL + u, slot - LAG
                    ahead = slot < SLOTS and not (last and u == UNROLL - 1)
                    if exists(LAG, slot, first, last):
                        take_result(n - LAG, done % SLOTS, batch_of(t, done), not first)
                    filling = first and slot < LAG
                    if not filling and exists(0, slot, first, last):
                        exponentials(n, slot, not first or slot > 2)
                    if filling and ONCE.get(slot) in BY_SCALAR:
                        empty_prologue(act, (ONCE[slot],), s_eva, act.copy, scaled)
                    if CT_AT <= j < CT_AT + NT and ahead:
                        act.wait_ge(s_ctj, NT * b + j - CT_AT + 1)
                        context_t_hi((u + 1) % 2, j - CT_AT, ps[:, JOB_BANK, :])
                    if filling:
                        exponentials(n, slot, slot > 2)
                    if exists(1, slot, first, last):
                        hi_part(n - 1, *previous(t, slot - 1), not first or slot > 2)
                    if CHI_AT <= j < CHI_AT + NT and ahead:
                        context_hi(b + 1, (u + 1) % 2, j - CHI_AT)
                    if first and slot == 0:
                        for g in range(NT):
                            context_hi(0, 0, g)
                    if first and NBLK + NT <= slot < NBLK + NT + NG:
                        g = slot - NBLK - NT
                        act.wait_ge(s_axs, 2)
                        act.activation(a16[:, HG * g:HG * g + HG, 0, :], a_sb[:, HG * g:HG * g + HG, :], ACT.Copy,
                                       scale=ax_scale[:, 0:1]).then_inc(s_16h, 1)
                    elif first and slot >= SLOTS - B // XG:
                        g = slot - SLOTS + B // XG
                        emptied(act, N_PRO - 1)
                        act.activation(x16[:, XG * g:XG * g + XG, 0, :], xT[:, XG * g:XG * g + XG, :], ACT.Copy,
                                       scale=ax_scale[:, 1:2]).then_inc(s_16h, 1)
                    if first and not filling and ONCE.get(slot) in BY_SCALAR:
                        empty_prologue(act, (ONCE[slot],), s_eva, act.copy, scaled)

            turns(act, step)

        @block.gpsimd
        def _(pool):
            pool.sem_inc(s_y, 1)
            pool.memset(ident[:, :], 0.0).then_inc(s_id0, 1)
            pool.wait_ge(s_id0, 1)
            pool.affine_select(out=ident[:, :], in_=ident[:, :], compare_op=ALU.not_equal, fill=1.0, base=0,
                               pattern=[[-1, P]], channel_multiplier=1).then_inc(s_ident, 1)
            pool.memset(c_raw[:, :, KT - 1, :], 0.0).then_inc(s_zero, 1)

            def split_parts(hi, lo, raw, count, s_done):
                pool.tensor_copy(hi, raw).then_inc(s_part, 1)
                wait_apart(pool, s_part, count)
                pool.tensor_tensor(lo, raw, hi.bitcast(F32), ALU.subtract).then_inc(s_done, 1)

            def context_top(b):
                wait_apart(pool, s_cm, b + 1)
                pool.partition_all_reduce(c_top[:, :], c_max[:, NT:NT + 1], P, RMAX).then_inc(s_ca, 1)

            def context_lo(b, par):
                wait_apart(pool, s_al, b + 1)
                flat = "p t d -> p (t d)"
                pool.tensor_scalar(c_scaled[:, :], c_raw[:, par, :, :].rearrange(flat), alpha[:, par:par + 1], 1.0,
                                   ALU.mult, ALU.mult).then_inc(s_cs, 1)
                wait_apart(pool, s_cs, b + 1)
                wait_apart(pool, s_chi, NT * b + NT)
                pool.tensor_tensor(c_hl[:, par, :, D:2 * D], c_scaled[:, :].rearrange("p (t d) -> p t d", d=D),
                                   c_hl[:, par, :, 0:D], ALU.subtract).then_inc(s_cl, 1)
                wait_apart(pool, s_cl, 2 * b + 1)
                pool.tensor_copy(c_tail[:, par, :], c_hl[:, par, KT - 1, D:2 * D]).then_inc(s_cl, 1)
                wait_apart(pool, s_cl, 2 * b + 2)
                pool.tensor_copy(c_tail[0:2 * KTAIL, par, :], c_hl[0:2 * KTAIL, par, KT - 1, 0:D]).then_inc(s_chl, 1)

            def split_queries(b, par, g):
                cols = slice(HG * QL * g, HG * QL * (g + 1))
                split_parts(g_hi[:, par, cols], g_lo[:, par, cols],
                            g_raw[:, HG * g:HG * g + HG, :].rearrange("p h q -> p (h q)"), NG * b + g + 1,
                            s_gs)

            def inverse_deviation(b, par):
                wait_apart(pool, s_ag, b + 1)
                pool.tensor_scalar(vpe[:, par:par + 1], mv[:, par, 1:2], EPS, None, ALU.add).then_inc(s_vp, 1)
                wait_apart(pool, s_vp, b + 1)
                pool.tensor_tensor(rstd[:, par:par + 1], vpe[:, par:par + 1], mhalf[:, :], ALU.pow).then_inc(s_rd, 1)

            def scale_rows(b, par, counted):
                wait_apart(pool, s_zn, b + 1)
                pool.tensor_tensor(zg[:, par, :], zn[:, par, :], rows_b[0:QL, 1, :], ALU.mult).then_inc(s_zg, 1)
                wait_apart(pool, s_zg, b + 1)
                if not isinstance(counted, int) or counted > 0:
                    wait_apart(pool, s_out[par], 16 * counted)
                pool.tensor_tensor(y[:, par, :], zg[:, par, :], rows_b[0:QL, 2, :], ALU.add).then_inc(s_y, 1)

            pool.wait_ge(s_bq, 16)
            for half in range(2):
                pool.wait_ge(s_w[1][half], 16)
            pool.tensor_tensor(wk_bq, w_raw[1], bq_wide, ALU.mult).then_inc(s_wb, 1)
            pool.wait_ge(s_bvl, 16)
            pool.tensor_copy(bv_wide[:, :, :],
                             bv_sb[:, :].unsqueeze(2).to_broadcast([P, PAIRS, P])).then_inc(s_bvw, 1)
            context_top(0)
            for g in range(1, NG):
                cols = slice(HG * QL * g, HG * QL * (g + 1))
                pool.wait_ge(s_part, g + 1)
                pool.tensor_tensor(g_lo[:, 0, cols], g_raw[:, HG * g:HG * g + HG, :].rearrange("p h q -> p (h q)"),
                                   g_hi[:, 0, cols].bitcast(F32),
                                   ALU.subtract).then_inc(s_gs, 1)
            context_lo(0, 0)

            def add_residual(a, e):
                pool.tensor_tensor(x_sb[:, a:e, :], x_sb[:, a:e, :], rows_b[0:QL, 0:1, :].to_broadcast([QL, e - a, D]),
                                   ALU.add).then_inc(s_xres, 1)

            def leave_lo(i, raw, parts, scale):
                n, w = raw.shape[1], raw.shape[2]
                scaled = c_scaled[:, 0:n * w].rearrange("p (n w) -> p n w", w=w)
                if i:
                    pool.wait_ge(s_16, i)
                pool.tensor_scalar(scaled, raw, scale, 1.0, ALU.mult, ALU.mult).then_inc(s_16s, 1)
                pool.wait_ge(s_16s, i + 1)
                pool.tensor_tensor(parts[:, :, 1, :], scaled, parts[:, :, 0, :], ALU.subtract).then_inc(s_16, 1)

            def step(t, first, last):
                for u in range(UNROLL):
                    b, other = t * UNROLL + u, (u + 1) % 2
                    if first and u == 1:
                        pool.wait_ge(s_axc, 1)
                        pool.partition_all_reduce(ax_top[:, :], ax_max[:, :], P, RMAX).then_inc(s_axa, 1)
                    if not (last and u == UNROLL - 1):
                        context_top(b + 1)
                    if not (first and u == 0):
                        inverse_deviation(b - 1, other)
                    if not (last and u == UNROLL - 1):
                        for g in range(2):
                            wait_apart(pool, s_gv, NG * b + g + 1)
                            split_queries(b + 1, other, g)
                    if not (first and u == 0):
                        scale_rows(b - 1, other, t)
                    if not (last and u == UNROLL - 1):
                        for g in range(2, NG):
                            wait_apart(pool, s_gv, NG * b + g + 1)
                            split_queries(b + 1, other, g)
                        context_lo(b + 1, other)
                    if first and u == 0:
                        emptied(pool, J_R)
                        add_residual(0, XG)
                    elif first:
                        emptied(pool, N_PRO - 1)
                        add_residual(XG, B)
                        pool.wait_ge(s_16h, NG + B // XG)
                        for i in range(2):
                            heads, batches = slice(i * H // 2, (i + 1) * H // 2), slice(i * B // 2, (i + 1) * B // 2)
                            leave_lo(2 * i, a_sb[:, heads, :], a16[:, heads], ax_scale[:, 0:1])
                            leave_lo(2 * i + 1, xT[:, batches, :], x16[:, batches], ax_scale[:, 1:2])
                        pool.wait_ge(s_16, 4)

            turns(pool, step)
            inverse_deviation(B - 1, (B - 1) % 2)
            scale_rows(B - 1, (B - 1) % 2, TURNS)


_INS = ['x', 'ctx_1024', 'L0_xattn_Wq', 'L0_xattn_bq', 'L0_xattn_Wk', 'L0_xattn_bk', 'L0_xattn_Wv', 'L0_xattn_bv',
        'L0_xattn_Wo', 'L0_xattn_bo', 'L0_xattn_gamma', 'L0_xattn_beta']
_OUTS = [((16, 100, 128), 'float32')]


def kernel(**inputs):
    import numpy as _np
    import concourse.bacc as _bacc
    from concourse import mybir as _mybir
    from concourse.bass_utils import run_bass_kernel_spmd as _run

    nc = _bacc.Bacc("TRN2", target_bir_lowering=False, num_devices=1)
    arrays, args = {}, []
    for name in _INS:
        a = _np.ascontiguousarray(inputs[name])
        arrays[f"in_{name}_dram"] = a
        args.append(nc.dram_tensor(f"in_{name}_dram", a.shape, _mybir.dt.from_np(a.dtype), kind="ExternalInput").ap())
    for i, (shape, dtype) in enumerate(_OUTS):
        dt = _mybir.dt.from_np(_np.dtype(dtype))
        args.append(nc.dram_tensor(f"out_{i}_dram", shape, dt, kind="ExternalOutput").ap())
    cross_attention_kernel(nc, *args)
    r = _run(nc, [arrays], core_ids=[0])
    got = tuple(r.results[0][f"out_{i}_dram"] for i in range(len(_OUTS)))
    return got[0]
```
